# Optimizing a Trainium2 kernel written in Bass

```python
import numpy as np
import jax
import jax.numpy as jnp

def _softmax(x, axis=-1):
    return jax.nn.softmax(x, axis=axis)

def _gelu(x):
    return jax.nn.gelu(x, approximate=True)

def _silu(x):
    return jax.nn.silu(x)

def _sigmoid(x):
    return jax.nn.sigmoid(x)

def _layernorm(x, axis=-1, eps=1e-05):
    m = jnp.mean(x, axis=axis, keepdims=True)
    v = jnp.var(x, axis=axis, keepdims=True)
    return (x - m) / jnp.sqrt(v + eps)

def _scatter_add(tgt, idx, src, axis=0):
    return tgt.at[idx].add(src)

def _segment_sum(src, seg, n):
    return jax.ops.segment_sum(src, seg, n)
kernel_name = 'mk_prb_d1_jaxref_r2_3a6c15'

def setup_inputs(seed: int=0):
    np.random.seed(seed)
    _w = jnp.asarray

    def _L0_attn_setup():
        import jax, jax.numpy as jnp
        import numpy as np
        B, T, DIM, HEADS, CF = (2, 2048, 512, 16, 4)

        def _compress(z, w, bias):
            y = jax.lax.conv_general_dilated(z.transpose(0, 2, 1), w, window_strides=(CF,), padding='VALID', dimension_numbers=('NCH', 'OIH', 'NCH'), feature_group_count=HEADS)
            return (y + bias[None, :, None]).transpose(0, 2, 1)
        key = jax.random.key(seed)
        ks = jax.random.split(key, 8)
        s = 0.02
        return {'x': jax.random.normal(ks[0], (B, T, DIM), jnp.float32), 'Wqkv': jax.random.normal(ks[1], (DIM, 3 * DIM), jnp.float32) * s, 'conv_w': jax.random.normal(ks[2], (DIM, DIM // HEADS, CF), jnp.float32) * s, 'conv_b': jax.random.normal(ks[3], (DIM,), jnp.float32) * s, 'null_k': jax.random.normal(ks[4], (1, 1, DIM), jnp.float32) * s, 'null_v': jax.random.normal(ks[5], (1, 1, DIM), jnp.float32) * s, 'W_out': jax.random.normal(ks[6], (DIM, DIM), jnp.float32) * s, 'b_out': jax.random.normal(ks[7], (DIM,), jnp.float32) * s}
    _L0_attn_in = _L0_attn_setup()

    def _L0_ffn_setup():
        import jax, jax.numpy as jnp
        import numpy as np
        B, T, C = (1, 2048, 512)
        E, K = (64, 8)
        G, TG = (8, 4)
        H, HS = (256, 1024)
        STD = 0.02

        def _route(xf, router_w, e_bias):
            S = xf.shape[0]
            scores = jax.nn.sigmoid(xf @ router_w.T)
            sb = scores + e_bias
            epg = E // G
            grp = jax.lax.top_k(sb.reshape(S, G, epg), K // TG)[0].sum(-1)
            gidx = jax.lax.top_k(grp, TG)[1]
            gmask = jnp.zeros((S, G), bool).at[jnp.arange(S)[:, None], gidx].set(True)
            emask = jnp.repeat(gmask, epg, axis=1)
            masked = jnp.where(emask, sb, -jnp.inf)
            topk_idx = jax.lax.top_k(masked, K)[1]
            w = jnp.take_along_axis(scores, topk_idx, axis=1)
            w = w / (w.sum(-1, keepdims=True) + 1e-20)
            return (topk_idx, w)
        key = jax.random.key(seed)
        ks = jax.random.split(key, 9)
        return {'x': jax.random.normal(ks[0], (B, T, C), jnp.float32), 'router_w': jax.random.normal(ks[1], (E, C), jnp.float32) * C ** (-0.5), 'e_bias': jnp.zeros((E,), jnp.float32), 'gate_w': jax.random.normal(ks[2], (E, C, H), jnp.float32) * STD, 'up_w': jax.random.normal(ks[3], (E, C, H), jnp.float32) * STD, 'down_w': jax.random.normal(ks[4], (E, H, C), jnp.float32) * STD, 'sh_gate_w': jax.random.normal(ks[5], (C, HS), jnp.float32) * STD, 'sh_up_w': jax.random.normal(ks[6], (C, HS), jnp.float32) * STD, 'sh_down_w': jax.random.normal(ks[7], (HS, C), jnp.float32) * STD}
    _L0_ffn_in = _L0_ffn_setup()
    _d = {'L0_attn_x': _L0_attn_in['x'], 'L0_attn_Wqkv': _L0_attn_in['Wqkv'], 'L0_attn_conv_w': _L0_attn_in['conv_w'], 'L0_attn_conv_b': _L0_attn_in['conv_b'], 'L0_attn_null_k': _L0_attn_in['null_k'], 'L0_attn_null_v': _L0_attn_in['null_v'], 'L0_attn_W_out': _L0_attn_in['W_out'], 'L0_attn_b_out': _L0_attn_in['b_out'], 'L0_ffn_router_w': _L0_ffn_in['router_w'], 'L0_ffn_e_bias': _L0_ffn_in['e_bias'], 'L0_ffn_gate_w': _L0_ffn_in['gate_w'], 'L0_ffn_up_w': _L0_ffn_in['up_w'], 'L0_ffn_down_w': _L0_ffn_in['down_w'], 'L0_ffn_sh_gate_w': _L0_ffn_in['sh_gate_w'], 'L0_ffn_sh_up_w': _L0_ffn_in['sh_up_w'], 'L0_ffn_sh_down_w': _L0_ffn_in['sh_down_w']}
    _x0 = _d['L0_attn_x']
    _d['L0_attn_x'] = jax.random.normal(jax.random.fold_in(jax.random.key(seed), 1), (4, 2048, 512), dtype=_x0.dtype)
    del _x0
    return _d

def reference(L0_attn_x, L0_attn_Wqkv, L0_attn_conv_w, L0_attn_conv_b, L0_attn_null_k, L0_attn_null_v, L0_attn_W_out, L0_attn_b_out, L0_ffn_router_w, L0_ffn_e_bias, L0_ffn_gate_w, L0_ffn_up_w, L0_ffn_down_w, L0_ffn_sh_gate_w, L0_ffn_sh_up_w, L0_ffn_sh_down_w):

    def _L0_attn_ref(x, Wqkv, conv_w, conv_b, null_k, null_v, W_out, b_out):
        import jax, jax.numpy as jnp
        import numpy as np
        B, T, DIM, HEADS, CF = (2, 2048, 512, 16, 4)

        def _compress(z, w, bias):
            y = jax.lax.conv_general_dilated(z.transpose(0, 2, 1), w, window_strides=(CF,), padding='VALID', dimension_numbers=('NCH', 'OIH', 'NCH'), feature_group_count=HEADS)
            return (y + bias[None, :, None]).transpose(0, 2, 1)
        b, t, d = x.shape
        h, cf = (HEADS, CF)
        dh = d // h
        qkv = x @ Wqkv
        q, k, v = jnp.split(qkv, 3, axis=-1)
        k = _compress(k, conv_w, conv_b)
        v = _compress(v, conv_w, conv_b)
        k = jnp.concatenate([jnp.broadcast_to(null_k, (b, 1, d)), k], axis=1)
        v = jnp.concatenate([jnp.broadcast_to(null_v, (b, 1, d)), v], axis=1)
        to_heads = lambda z: z.reshape(b, z.shape[1], h, dh).transpose(0, 2, 1, 3)
        q, k, v = (to_heads(q), to_heads(k), to_heads(v))
        dots = jnp.einsum('bhid,bhjd->bhij', q, k) * d ** (-0.5)
        mask_value = -jnp.finfo(dots.dtype).max
        q_idx = jnp.arange(t)
        k_idx = jnp.arange(t).reshape(-1, cf).max(axis=-1)
        mask = q_idx[:, None] < k_idx[None, :]
        mask = jnp.pad(mask, ((0, 0), (1, 0)), constant_values=False)
        dots = jnp.where(mask[None, None], mask_value, dots)
        attn = jax.nn.softmax(dots, axis=-1)
        out = jnp.einsum('bhij,bhjd->bhid', attn, v)
        out = out.transpose(0, 2, 1, 3).reshape(b, t, d)
        out = out @ W_out + b_out
        out = jnp.fft.fft(jnp.fft.fft(out.astype(jnp.float32), axis=-1), axis=-2).real
        return out

    def _L0_ffn_ref(x, router_w, e_bias, gate_w, up_w, down_w, sh_gate_w, sh_up_w, sh_down_w):
        import jax, jax.numpy as jnp
        import numpy as np
        B, T, C = (1, 2048, 512)
        E, K = (64, 8)
        G, TG = (8, 4)
        H, HS = (256, 1024)
        STD = 0.02

        def _route(xf, router_w, e_bias):
            S = xf.shape[0]
            scores = jax.nn.sigmoid(xf @ router_w.T)
            sb = scores + e_bias
            epg = E // G
            grp = jax.lax.top_k(sb.reshape(S, G, epg), K // TG)[0].sum(-1)
            gidx = jax.lax.top_k(grp, TG)[1]
            gmask = jnp.zeros((S, G), bool).at[jnp.arange(S)[:, None], gidx].set(True)
            emask = jnp.repeat(gmask, epg, axis=1)
            masked = jnp.where(emask, sb, -jnp.inf)
            topk_idx = jax.lax.top_k(masked, K)[1]
            w = jnp.take_along_axis(scores, topk_idx, axis=1)
            w = w / (w.sum(-1, keepdims=True) + 1e-20)
            return (topk_idx, w)
        Bq, Tq, Cq = x.shape
        xf = x.reshape(Bq * Tq, Cq)
        shared = jax.nn.silu(xf @ sh_gate_w) * (xf @ sh_up_w) @ sh_down_w
        topk_idx, w = _route(xf, router_w, e_bias)
        fe = topk_idx.reshape(-1)
        order = jnp.argsort(fe, stable=True)
        tok = order // K
        sorted_x = xf[tok]
        group_sizes = jnp.bincount(fe, length=E).astype(jnp.int32)
        g = jax.lax.ragged_dot(sorted_x, gate_w, group_sizes)
        u = jax.lax.ragged_dot(sorted_x, up_w, group_sizes)
        h = jax.nn.silu(g) * u
        o = jax.lax.ragged_dot(h, down_w, group_sizes)
        o = o * w.reshape(-1)[order][:, None]
        routed = jnp.zeros_like(xf).at[tok].add(o)
        return (shared + routed).reshape(Bq, Tq, Cq)
    x = L0_attn_x
    xn = _layernorm(x, axis=-1)
    x = x + _L0_attn_ref(xn, L0_attn_Wqkv, L0_attn_conv_w, L0_attn_conv_b, L0_attn_null_k, L0_attn_null_v, L0_attn_W_out, L0_attn_b_out) + _L0_ffn_ref(xn, L0_ffn_router_w, L0_ffn_e_bias, L0_ffn_gate_w, L0_ffn_up_w, L0_ffn_down_w, L0_ffn_sh_gate_w, L0_ffn_sh_up_w, L0_ffn_sh_down_w)
    return x

_drawn_inputs = setup_inputs


def setup_inputs(seed=0):
    import zlib

    import numpy as np

    out = dict(_drawn_inputs(seed))
    spreads = {'L0_ffn_e_bias': (0.0, 0.8)}
    factors = {'L0_attn_null_k': 64.0,
     'L0_ffn_router_w': 8.0,
     'L0_ffn_gate_w': 8.0,
     'L0_ffn_up_w': 8.0,
     'L0_ffn_down_w': 8.0,
     'L0_ffn_sh_gate_w': 8.0,
     'L0_ffn_sh_up_w': 8.0,
     'L0_ffn_sh_down_w': 8.0,
     'L0_attn_null_v': 8.0}
    for name, (base, spread) in spreads.items():
        noise = np.random.default_rng([zlib.crc32(name.encode()), seed]).standard_normal(out[name].shape)
        drawn = base * np.exp(spread * noise) if base else spread * noise
        out[name] = jnp.asarray(drawn.astype(out[name].dtype))
    for name, factor in factors.items():
        out[name] = (out[name] * factor).astype(out[name].dtype)
    return out
```

```python
from contextlib import ExitStack

import numpy as np

import concourse.bass as bass
from concourse import mybir

F32 = mybir.dt.float32
BF16 = mybir.dt.bfloat16
I32 = mybir.dt.int32
ALU = mybir.AluOpType
ACT = mybir.ActivationFunctionType
AX = mybir.AxisListType.X

P = 128
BATCH, SEQ, DIM = 4, 2048, 512
TOK = BATCH * SEQ
HEADS, DH, CF = 16, 32, 4
NC = SEQ // CF
DC = DIM // P
HPC = P // DH
EXPERTS, TOPK, GROUPS, TOPG = 64, 8, 8, 4
EPG = EXPERTS // GROUPS
HID, HSH = 256, 1024
EPS = 1e-5
SCALE = float(DIM) ** -0.5
BIG = 1e30

TB = 512
TPB = TB // P
NSTEP = TOK // TB
NTILE = TOK // P
CPB = TB // CF

RB = 256
RT = RB // P
SLOTS_USED = TOK * TOPK
NBLK = -(-(SLOTS_USED // RB + EXPERTS - 1) // 2) * 2
NSLOT = NBLK * RB
NCOL = NSLOT // P


def hold(eng, sem, value, passed):
    eng.wait_ge(sem, value)
    eng.sem_inc(passed, 1)


class Steps:

    def __init__(self, eng, sem, base, passed=None):
        self.eng, self.sem, self.base, self.passed, self.n = eng, sem, base, passed, 0

    def mark(self, instruction):
        instruction.then_inc(self.sem, 1)
        self.n += 1
        return instruction

    def wait(self):
        self.eng.wait_ge(self.sem, self.base + self.n)

    def hold(self):
        hold(self.eng, self.sem, self.base + self.n, self.passed)


def opener(nc, ctx, tag=""):
    def sb(name, shape, dt=F32):
        return ctx.enter_context(nc.sbuf_tensor(tag + name, shape, dt))

    def ps(name, shape, dt=F32):
        return ctx.enter_context(nc.psum_tensor(tag + name, shape, dt))

    def sem(name):
        return ctx.enter_context(nc.semaphore(tag + name))

    return sb, ps, sem



A_ORDER = ([("xT", i) for i in range(4)] + [("down", i) for i in range(4)] + [("router", 0)]
           + [("qkv", i) for i in range(12)] + [("kc", 0), ("vc", 0)]
           + [("gu", i) for i in range(16)] + [("pos", 0)])
A_PER = {"xT": 4, "down": 4, "router": 1, "qkv": 12, "kc": 1, "vc": 1, "gu": 16, "pos": 1}


def stage_a(nc, t):
    ctx = ExitStack()
    with ctx:
        sb, ps, sem = opener(nc, ctx)
        wqkv = sb("a_wqkv", [P, DC, 3 * DIM])
        wrt = sb("a_wrt", [P, DC, EXPERTS])
        wconv = sb("a_wconv", [P, DC, CF, P])
        wsg = sb("a_wsg", [P, DC, HSH])
        wsu = sb("a_wsu", [P, DC, HSH])
        wsd = sb("a_wsd", [P, HSH // P, DIM])
        kbias = sb("a_kbias", [P, DC])
        vbias = sb("a_vbias", [P, DIM])
        ebias = sb("a_ebias", [P, EXPERTS])
        ident = sb("a_ident", [P, P])
        trif = sb("a_trif", [P, P])
        tri = sb("a_tri", [P, P], BF16)
        ones = sb("a_ones", [P, P], BF16)
        before = sb("a_before", [P, GROUPS, GROUPS])
        mhalf = sb("a_mhalf", [P, TPB])
        x = sb("a_x", [P, TPB, DIM])
        xn = sb("a_xn", [P, TPB, DIM])
        xT = sb("a_xT", [P, DC, TB])
        qs = sb("a_qs", [P, DC, TB])
        ks = sb("a_ks", [P, DC, CF, CPB])
        vs = sb("a_vs", [P, DC, CF, CPB])
        kcs = sb("a_kcs", [P, DC, CPB])
        vcs = sb("a_vcs", [P, DIM])
        sg = sb("a_sg", [P, 2, TB])
        gated = sb("a_gated", [P, 2, TB])
        hT = sb("a_hT", [P, HSH // P, TB])
        shs = sb("a_shs", [P, TPB, DIM])
        stats = sb("a_stats", [P, TPB, 6])
        mv = sb("a_mv", [P, TPB, 2])
        ve = sb("a_ve", [P, TPB])
        y0 = sb("a_y0", [P, TPB])
        ya = sb("a_ya", [P, TPB])
        yb = sb("a_yb", [P, TPB])
        rstd = sb("a_rstd", [P, TPB])
        NG = TPB * GROUPS
        sc = sb("a_sc", [P, TPB, EXPERTS])
        sbi = sb("a_sbi", [P, TPB, EXPERTS])
        hi4 = sb("a_hi4", [P, NG, 4])
        lo4 = sb("a_lo4", [P, NG, 4])
        hi2 = sb("a_hi2", [P, NG, 2])
        lo2 = sb("a_lo2", [P, NG, 2])
        mi2 = sb("a_mi2", [P, NG, 2])
        hi1 = sb("a_hi1", [P, NG])
        lo1 = sb("a_lo1", [P, NG])
        mi1 = sb("a_mi1", [P, NG])
        grp = sb("a_grp", [P, NG])
        cgt = sb("a_cgt", [P, TPB, GROUPS, GROUPS])
        ceq = sb("a_ceq", [P, TPB, GROUPS, GROUPS])
        rank = sb("a_rank", [P, NG])
        gkeep = sb("a_gkeep", [P, NG])
        masked = sb("a_masked", [P, TPB, EXPERTS])
        best = sb("a_best", [P, TPB, 8])
        taken = sb("a_taken", [P, TPB, EXPERTS])
        sel = sb("a_sel", [P, TPB, EXPERTS])
        selb = sb("a_selb", [P, TPB, EXPERTS], BF16)
        wsum = sb("a_wsum", [P, TPB])
        winv = sb("a_winv", [P, TPB])
        w = sb("a_w", [P, TPB, EXPERTS])
        posm = sb("a_posm", [P, TPB, EXPERTS])
        ptmp = sb("a_ptmp", [P, TPB, EXPERTS])
        carry = sb("a_carry", [P, EXPERTS])
        bank = [ps(f"a_bank{i}", [P, 512]) for i in range(8)]

        w_in = sem("a_w_in")
        x_in = sem("a_x_in")
        passed = sem("a_passed")
        const_ready = sem("a_const_ready")
        dve_done = sem("a_dve_done")
        var_ready = sem("a_var_ready")
        pow_ready = sem("a_pow_ready")
        xn_ready = sem("a_xn_ready")
        route_ready = sem("a_route_ready")
        scores_ready = sem("a_scores_ready")
        sig_ready = sem("a_sig_ready")
        hT_ready = sem("a_hT_ready")
        xn_out = sem("a_xn_out")
        q_out = sem("a_q_out")
        kc_out = sem("a_kc_out")
        vc_out = sem("a_vc_out")
        wp_out = sem("a_wp_out")
        sh_out = sem("a_sh_out")
        cnt_out = sem("a_cnt_out")
        filled = {k: sem(f"a_filled_{k}") for k in A_PER}
        emptied = {k: sem(f"a_emptied_{k}") for k in A_PER}

        def nth(kind, step, i):
            done_before = (step - 1 if kind == "down" else step) * A_PER[kind]
            return done_before + i + 1

        NLOADS = 14
        block = ctx.enter_context(nc.Block())

        @block.sync
        def _(sp):
            for dst, src in ((wqkv, t["wqkv"]), (wsg, t["sh_gate"]), (wsu, t["sh_up"]), (wsd, t["sh_down"]), (wrt, t["router_t"])):
                sp.dma_start(dst[:, :, :], src.rearrange("(k p) n -> p k n", p=P)).then_inc(w_in, 16)
            sp.dma_start(wconv[:, :, :, :], t["conv_bd"]).then_inc(w_in, 16)
            for dst, src in ((kbias, t["conv_b_col"]), (vbias, t["conv_b_row"]), (ebias, t["e_bias_row"]), (ident, t["ident"]),
                             (trif, t["tri"])):
                sp.dma_start(dst[:, :], src).then_inc(w_in, 16)
            sp.dma_start(before[:, :, :], t["before"]).then_inc(w_in, 16)
            sp.dma_start(mhalf[:, :], t["mhalf"]).then_inc(w_in, 16)
            sp.dma_start(sel[:, :, :].rearrange("p a e -> p (a e)")[:, 0:P], t["ones"]).then_inc(w_in, 16)

            def load_x(s):
                sp.dma_start(x[:, :, :], t["x"][bass.ds(s * TB, TB), :].rearrange("(i p) c -> p i c", p=P))\
                    .then_inc(x_in, 16)

            def step(s, first, last):
                if not last:
                    hold(sp, xn_ready, (s + 1) * TPB, passed)
                    load_x(s + 1)
                else:
                    hold(sp, xn_ready, (s + 1) * TPB, passed)
                sp.dma_start(t["xn"][bass.ds(s * TB, TB), :].rearrange("(i p) c -> p i c", p=P), xn[:, :, :])\
                    .then_inc(xn_out, 16)
                if not first:
                    store_shared(s - 1)
                hold(sp, emptied["qkv"], nth("qkv", s, 3), passed)
                sp.dma_start(t["q"][:, :, bass.ds(s * TB, TB)].rearrange("c p n -> p c n"), qs[:, :, :]).then_inc(q_out, 16)
                hold(sp, emptied["kc"], nth("kc", s, 0), passed)
                sp.dma_start(t["kc"][:, :, bass.ds(s * CPB, CPB)].rearrange("c p n -> p c n"), kcs[:, :, :])\
                    .then_inc(kc_out, 16)
                hold(sp, emptied["vc"], nth("vc", s, 0), passed)
                sp.dma_start(t["vc"][bass.ds(s * CPB, CPB), :], vcs[:, :]).then_inc(vc_out, 16)
                hold(sp, emptied["pos"], nth("pos", s, 0), passed)
                sp.dma_start(t["pos"][:, bass.ds(s * TPB * EXPERTS, TPB * EXPERTS)],
                             posm[:, :, :].rearrange("p a e -> p (a e)")).then_inc(wp_out, 16)
                sp.dma_start(t["w"][:, bass.ds(s * TPB * EXPERTS, TPB * EXPERTS)],
                             w[:, :, :].rearrange("p a e -> p (a e)")).then_inc(wp_out, 16)

            def store_shared(s):
                hold(sp, emptied["down"], (s + 1) * 4, passed)
                sp.dma_start(t["shared"][bass.ds(s * TB, TB), :].rearrange("(i p) c -> p i c", p=P), shs[:, :, :])\
                    .then_inc(sh_out, 16)

            load_x(0)
            step(0, True, False)
            with sp.Fori(1, NSTEP - 1) as s:
                step(s, False, False)
            step(NSTEP - 1, False, True)
            store_shared(NSTEP - 1)
            sp.dma_start(t["cnt"], carry[:, :]).then_inc(cnt_out, 16)
            for s_, n in ((xn_out, 1), (q_out, 1), (kc_out, 1), (vc_out, 1), (wp_out, 2), (sh_out, 1)):
                sp.wait_ge(s_, 16 * n * NSTEP)
            sp.wait_ge(cnt_out, 16)

        @block.gpsimd
        def _(pool):
            pool.wait_ge(w_in, 16 * NLOADS)

            def inv_sqrt(s):
                pool.wait_ge(var_ready, s + 1)
                pool.tensor_tensor(y0[:, :], ve[:, :], mhalf[:, :], ALU.pow).then_inc(pow_ready, 1)

            inv_sqrt(0)
            with pool.Fori(1, NSTEP) as s:
                inv_sqrt(s)

        @block.scalar
        def _(act):
            def step(s, first, last):
                for k in range(DC):
                    act.wait_ge(filled["xT"], nth("xT", s, k))
                    act.copy(xT[:, k, :], bank[k][:, :]).then_inc(emptied["xT"], 1)
                act.wait_ge(filled["router"], nth("router", s, 0))
                if not first:
                    act.wait_ge(route_ready, s)
                act.activation(sc[:, :, :].rearrange("p a e -> p (a e)"), bank[A_BANK[("router", 0)]][:, 0:TPB * EXPERTS],
                               ACT.Sigmoid).then_inc(emptied["router"], 1)
                for i in range(12):
                    act.wait_ge(filled["qkv"], nth("qkv", s, i))
                    src = bank[A_BANK[("qkv", i)]]
                    if i == 0 and not first:
                        act.wait_ge(q_out, 16 * s)
                    if i < 4:
                        act.copy(qs[:, i, :], src[:, :]).then_inc(emptied["qkv"], 1)
                    else:
                        dst = ks if i < 8 else vs
                        act.copy(dst[:, i % 4, :, :], src[:, :].rearrange("p (j c) -> p c j", c=CF))\
                            .then_inc(emptied["qkv"], 1)
                act.wait_ge(filled["kc"], nth("kc", s, 0))
                if not first:
                    act.wait_ge(kc_out, 16 * s)
                for k in range(DC):
                    last_i = act.activation(kcs[:, k, :], bank[A_BANK[("kc", 0)]][:, k * CPB:(k + 1) * CPB], ACT.Identity,
                                            bias=kbias[:, k:k + 1])
                last_i.then_inc(emptied["kc"], 1)
                for j in range(8):
                    act.wait_ge(filled["gu"], nth("gu", s, 2 * j))
                    if j >= 2 or not first:
                        act.wait_ge(emptied["gu"], nth("gu", s, 2 * j - 3))
                    act.activation(sg[:, j % 2, :], bank[A_BANK[("gu", 2 * j)]][:, :], ACT.Sigmoid)\
                        .then_inc(sig_ready, 1)

            act.wait_ge(w_in, 16 * NLOADS)
            step(0, True, False)
            with act.Fori(1, NSTEP) as s:
                step(s, False, False)

        @block.vector
        def _(dve):
            def layernorm(s, st, first):
                dve.wait_ge(x_in, 16 * (s + 1))
                for i in range(TPB):
                    st.mark(dve.bn_stats(stats[:, i, :], x[:, i, :]))
                st.hold()
                for i in range(TPB):
                    st.mark(dve.bn_aggr(mv[:, i, :], stats[:, i, :]))
                st.wait()
                dve.tensor_scalar(ve[:, :], mv[:, :, 1], EPS, None, ALU.add).then_inc(var_ready, 1)
                dve.wait_ge(pow_ready, s + 1)
                st.mark(dve.tensor_tensor(ya[:, :], y0[:, :], y0[:, :], ALU.mult))
                st.wait()
                st.mark(dve.tensor_tensor(yb[:, :], ya[:, :], ve[:, :], ALU.mult))
                st.wait()
                st.mark(dve.tensor_scalar(ya[:, :], yb[:, :], -0.5, 1.5, ALU.mult, ALU.add))
                st.wait()
                st.mark(dve.tensor_tensor(rstd[:, :], ya[:, :], y0[:, :], ALU.mult))
                st.wait()
                if not first:
                    dve.wait_ge(filled["xT"], 4 * s)
                    dve.wait_ge(xn_out, 16 * s)
                for i in range(TPB):
                    dve.tensor_scalar(xn[:, i, :], x[:, i, :], mv[:, i, 0:1], rstd[:, i:i + 1], ALU.subtract, ALU.mult)\
                        .then_inc(xn_ready, 1)

            def route(s, st, first):
                def tt(out, a, b, op):
                    return st.mark(dve.tensor_tensor(out, a, b, op))

                dve.wait_ge(emptied["router"], nth("router", s, 0))
                tt(sbi[:, :, :], sc[:, :, :], ebias[:, None, :].broadcast_to([P, TPB, EXPERTS]), ALU.add)
                st.wait()
                v = sbi[:, :, :].rearrange("p a (g e) -> p (a g) e", e=EPG)
                tt(hi4[:, :, :], v[:, :, 0:4], v[:, :, 4:8], ALU.max)
                tt(lo4[:, :, :], v[:, :, 0:4], v[:, :, 4:8], ALU.min)
                st.wait()
                tt(hi2[:, :, :], hi4[:, :, 0:2], hi4[:, :, 2:4], ALU.max)
                tt(mi2[:, :, :], hi4[:, :, 0:2], hi4[:, :, 2:4], ALU.min)
                tt(lo2[:, :, :], lo4[:, :, 0:2], lo4[:, :, 2:4], ALU.max)
                st.wait()
                tt(lo2[:, :, :], lo2[:, :, :], mi2[:, :, :], ALU.max)
                tt(hi1[:, :], hi2[:, :, 0], hi2[:, :, 1], ALU.max)
                tt(mi1[:, :], hi2[:, :, 0], hi2[:, :, 1], ALU.min)
                st.wait()
                tt(lo1[:, :], lo2[:, :, 0], lo2[:, :, 1], ALU.max)
                st.wait()
                tt(lo1[:, :], lo1[:, :], mi1[:, :], ALU.max)
                st.wait()
                tt(grp[:, :], hi1[:, :], lo1[:, :], ALU.add)
                st.wait()
                shape = [P, TPB, GROUPS, GROUPS]
                g3 = grp[:, :].rearrange("p (a g) -> p a g", g=GROUPS)
                other = g3[:, :, None, :].broadcast_to(shape)
                own = g3[:, :, :, None].broadcast_to(shape)
                tt(cgt[:, :, :, :], other, own, ALU.is_gt)
                tt(ceq[:, :, :, :], other, own, ALU.is_equal)
                st.wait()
                tt(ceq[:, :, :, :], ceq[:, :, :, :], before[:, None, :, :].broadcast_to(shape), ALU.mult)
                st.wait()
                tt(cgt[:, :, :, :], cgt[:, :, :, :], ceq[:, :, :, :], ALU.add)
                st.wait()
                st.mark(dve.tensor_reduce(rank[:, :], cgt[:, :, :, :].rearrange("p a g o -> p (a g) o"), AX, ALU.add))
                st.wait()
                st.mark(dve.tensor_scalar(gkeep[:, :], rank[:, :], float(TOPG), -1.0, ALU.is_lt, ALU.add))
                st.wait()
                st.mark(dve.scalar_tensor_tensor(
                    masked[:, :, :].rearrange("p a (g e) -> p (a g) e", e=EPG),
                    gkeep[:, :, None].broadcast_to([P, NG, EPG]), BIG, v, ALU.mult, ALU.add))
                st.hold()
                for i in range(TPB):
                    st.mark(dve.max(best[:, i, :], masked[:, i, :]))
                st.hold()
                for i in range(TPB):
                    st.mark(dve.match_replace(taken[:, i, :], best[:, i, :], masked[:, i, :], -3e38))
                st.wait()
                if not first:
                    dve.wait_ge(wp_out, 32 * s)
                tt(sel[:, :, :], taken[:, :, :], masked[:, :, :], ALU.not_equal)
                st.wait()
                st.mark(dve.tensor_copy(selb[:, :, :], sel[:, :, :]))
                tt(w[:, :, :], sc[:, :, :], sel[:, :, :], ALU.mult)
                st.wait()
                st.mark(dve.tensor_reduce(wsum[:, :], w[:, :, :], AX, ALU.add))
                st.wait()
                st.mark(dve.tensor_scalar(wsum[:, :], wsum[:, :], 1e-20, None, ALU.add))
                st.wait()
                st.mark(dve.reciprocal(winv[:, :], wsum[:, :]))
                st.wait()
                dve.tensor_tensor(w[:, :, :], w[:, :, :], winv[:, :, None].broadcast_to([P, TPB, EXPERTS]), ALU.mult)\
                    .then_inc(route_ready, 1)

            def down_out(s, first):
                for i in range(4):
                    dve.wait_ge(filled["down"], 4 * s + i + 1)
                    if i == 0 and not first:
                        dve.wait_ge(sh_out, 16 * s)
                    dve.tensor_copy(shs[:, i, :], bank[A_BANK[("down", i)]][:, :]).then_inc(emptied["down"], 1)

            def step(s, first, last, second=False):
                st = Steps(dve, dve_done, s * STEP_MARKS + LN_MARKS + 3, passed)
                if not first:
                    down_out(s - 1, second)
                if not last:
                    layernorm(s + 1, st, False)
                route(s, st, first)
                dve.wait_ge(filled["vc"], nth("vc", s, 0))
                if not first:
                    dve.wait_ge(vc_out, 16 * s)
                dve.tensor_tensor(vcs[:, :], bank[A_BANK[("vc", 0)]][:, :], vbias[:, :], ALU.add)\
                    .then_inc(emptied["vc"], 1)
                for j in range(8):
                    dve.wait_ge(sig_ready, s * 8 + j + 1)
                    dve.tensor_tensor(gated[:, j % 2, :], sg[:, j % 2, :], bank[A_BANK[("gu", 2 * j)]][:, :], ALU.mult)\
                        .then_inc(emptied["gu"], 1)
                    dve.wait_ge(filled["gu"], nth("gu", s, 2 * j + 1))
                    dve.wait_ge(emptied["gu"], nth("gu", s, 2 * j))
                    if j == 0 and not first:
                        dve.wait_ge(filled["down"], nth("down", s, 3))
                    dve.tensor_tensor(hT[:, j, :], gated[:, j % 2, :], bank[A_BANK[("gu", 2 * j + 1)]][:, :], ALU.mult)\
                        .then_inc(emptied["gu"], 1)
                dve.wait_ge(filled["pos"], nth("pos", s, 0))
                pb = bank[A_BANK[("pos", 0)]]
                st.mark(dve.scalar_tensor_tensor(
                    ptmp[:, :, :], pb[:, 0:TPB * EXPERTS].rearrange("p (a e) -> p a e", a=TPB), 1.0,
                    carry[:, None, :].broadcast_to([P, TPB, EXPERTS]), ALU.add, ALU.add))
                st.wait()
                st.mark(dve.tensor_tensor(posm[:, :, :], ptmp[:, :, :], sel[:, :, :], ALU.mult))
                st.mark(dve.tensor_tensor(carry[:, :], carry[:, :], pb[:, TPB * EXPERTS:(TPB + 1) * EXPERTS], ALU.add))
                st.wait()
                dve.sem_inc(emptied["pos"], 1)
                if last:
                    assert st.n == STEP_MARKS - LN_MARKS, st.n
                else:
                    assert st.n == STEP_MARKS, st.n

            LN_MARKS = 2 * TPB + 4
            STEP_MARKS = LN_MARKS + 28 + 2 * TPB
            dve.wait_ge(w_in, 16 * NLOADS)
            s0 = Steps(dve, dve_done, 0, passed)
            s0.mark(dve.memset(carry[:, :], 0.0))
            s0.mark(dve.tensor_copy(ones[:, :], sel[:, :, :].rearrange("p a e -> p (a e)")[:, 0:P]))
            s0.mark(dve.tensor_copy(tri[:, :], trif[:, :]))
            s0.wait()
            dve.sem_inc(const_ready, 1)
            layernorm(0, s0, True)
            step(0, True, False)
            step(1, False, False, second=True)
            with dve.Fori(2, NSTEP - 1) as s:
                step(s, False, False)
            step(NSTEP - 1, False, True)
            down_out(NSTEP - 1, False)

        @block.tensor
        def _(pe):
            def bank_free(kind, i, s, first):
                g = A_ORDER.index((kind, i))
                if g >= 8:
                    k, o = A_ORDER[g - 8]
                    if not (first and k == "down"):
                        pe.wait_ge(emptied[k], nth(k, s, o))
                elif not first:
                    k, o = A_ORDER[g + len(A_ORDER) - 8]
                    pe.wait_ge(emptied[k], nth(k, s - 1, o))
                return bank[A_BANK[(kind, i)]]

            def down(s, first, bank_wait):
                pe.wait_ge(emptied["gu"], 16 * (s + 1))
                for i in range(TPB):
                    b = bank_wait(i)
                    for j in range(HSH // P):
                        last_i = pe.matmul(b[:, :], hT[:, j, i * P:(i + 1) * P], wsd[:, j, :], start=j == 0,
                                           stop=j == HSH // P - 1)
                    last_i.then_inc(filled["down"], 1)

            def step(s, first):
                for k in range(DC):
                    b = bank_free("xT", k, s, first)
                    if k == 0:
                        pe.wait_ge(xn_ready, TPB * (s + 1))
                    for i in range(TPB):
                        last_i = pe.transpose(b[:, i * P:(i + 1) * P], xn[:, i, k * P:(k + 1) * P], ident[:, :])
                    last_i.then_inc(filled["xT"], 1)
                if not first:
                    down(s - 1, False, lambda i: bank_free("down", i, s, False))
                b = bank_free("router", 0, s, first)
                pe.wait_ge(emptied["xT"], nth("xT", s, DC - 1))
                for i in range(TPB):
                    for k in range(DC):
                        last_i = pe.matmul(b[:, i * EXPERTS:(i + 1) * EXPERTS], xT[:, k, i * P:(i + 1) * P], wrt[:, k, :],
                                           start=k == 0, stop=k == DC - 1)
                last_i.then_inc(filled["router"], 1)
                for m in range(12):
                    b = bank_free("qkv", m, s, first)
                    for k in range(DC):
                        last_i = pe.matmul(b[:, :], wqkv[:, k, m * P:(m + 1) * P], xT[:, k, :], start=k == 0,
                                           stop=k == DC - 1)
                    last_i.then_inc(filled["qkv"], 1)
                b = bank_free("kc", 0, s, first)
                pe.wait_ge(emptied["qkv"], nth("qkv", s, 11))
                for k in range(DC):
                    for c in range(CF):
                        last_i = pe.matmul(b[:, k * CPB:(k + 1) * CPB], wconv[:, k, c, :], ks[:, k, c, :], start=c == 0,
                                           stop=c == CF - 1)
                last_i.then_inc(filled["kc"], 1)
                b = bank_free("vc", 0, s, first)
                for k in range(DC):
                    for c in range(CF):
                        last_i = pe.matmul(b[:, k * P:(k + 1) * P], vs[:, k, c, :], wconv[:, k, c, :], start=c == 0,
                                           stop=c == CF - 1)
                last_i.then_inc(filled["vc"], 1)
                for j in range(HSH // P):
                    for i, wt in ((2 * j, wsg), (2 * j + 1, wsu)):
                        b = bank_free("gu", i, s, first)
                        for k in range(DC):
                            last_i = pe.matmul(b[:, :], wt[:, k, j * P:(j + 1) * P], xT[:, k, :], start=k == 0,
                                               stop=k == DC - 1)
                        last_i.then_inc(filled["gu"], 1)
                b = bank_free("pos", 0, s, first)
                pe.wait_ge(route_ready, s + 1)
                for i in range(TPB + 1):
                    dst = b[:, i * EXPERTS:(i + 1) * EXPERTS]
                    for n in range(min(i + 1, TPB)):
                        last_i = pe.matmul(dst, (tri if n == i else ones)[:, :], selb[:, n, :], start=n == 0,
                                           stop=n == min(i + 1, TPB) - 1)
                last_i.then_inc(filled["pos"], 1)

            pe.wait_ge(w_in, 16 * NLOADS)
            pe.wait_ge(const_ready, 1)
            step(0, True)
            with pe.Fori(1, NSTEP) as s:
                step(s, False)
            down(NSTEP - 1, False, lambda i: bank_free("down", i, NSTEP, False))


A_BANK = {g: i % 8 for i, g in enumerate(A_ORDER)}




KW = P // CF
QT = SEQ // P
PAIRS = HPC // 2
UNITS = QT * PAIRS


class Attention:

    def __init__(self, nc, ctx, t, b0, nb, tag):
        self.t, self.b0, self.nb, self.items = t, b0, nb, nb * DC
        sb, ps, sem = opener(nc, ctx, tag)
        self.q = [sb(f"q{s}", [P, SEQ]) for s in range(2)]
        self.kc = [sb(f"kc{s}", [P, NC]) for s in range(2)]
        self.vc = [sb(f"vc{s}", [P, NC // P, P]) for s in range(2)]
        self.nk = [sb(f"nk{s}", [P, HPC]) for s in range(2)]
        self.nullv = sb("nullv", [P, DIM])
        self.late = sb("late", [P, KW])
        self.ident = sb("ident", [P, P])
        self.p = [sb(f"p{r}", [P, 2, NC]) for r in range(2)]
        self.pT = [sb(f"pT{r}", [P, 2, NC]) for r in range(2)]
        self.mx = sb("mx", [P, 2, 2])
        self.s0n = [sb(f"s0n{s}", [P, QT, HPC]) for s in range(2)]
        self.nm = [sb(f"nm{s}", [P, QT, HPC]) for s in range(2)]
        self.rs = [sb(f"rs{s}", [P, QT, HPC]) for s in range(2)]
        self.d0 = sb("d0", [P, QT, HPC])
        self.p0 = sb("pnull", [P, QT, HPC])
        self.den = sb("den", [P, QT, HPC])
        self.rden = sb("rden", [P, QT, HPC])
        self.raw = [sb(f"raw{s}", [P, QT, P]) for s in range(2)]
        self.nulls = sb("nulls", [P, QT, P])
        self.ps_s = [ps(f"ps_s{r}", [P, 2, 512]) for r in range(2)]
        self.ps_t = [ps(f"ps_t{h}", [P, 512]) for h in range(2)]
        self.ps_o = [ps(f"ps_o{r}", [P, 512]) for r in range(2)]
        self.const_in = sem("const_in")
        self.item_in = [sem(f"item_in{s}") for s in range(2)]
        self.zeroed = sem("zeroed")
        self.passed = sem("passed")
        self.s0_filled = sem("s0_filled")
        self.s0_emptied = sem("s0_emptied")
        self.s_filled = sem("s_filled")
        self.s_emptied = sem("s_emptied")
        self.nm_ready = sem("nm_ready")
        self.p_transposed = sem("p_transposed")
        self.t0_emptied = sem("t0_emptied")
        self.t1_emptied = sem("t1_emptied")
        self.pv_done = sem("pv_done")
        self.o_emptied = sem("o_emptied")
        self.dve_done = sem("dve_done")
        self.d0_ready = sem("d0_ready")
        self.p0_ready = sem("p0_ready")
        self.raw_ready = sem("raw_ready")
        self.att_out = [sem(f"att_out{s}") for s in range(2)]

    def each_item(self, eng):
        with eng.Fori(0, self.nb) as b:
            with eng.Fori(0, DC // 2) as c2:
                for s in range(2):
                    yield s, b * DC + c2 * 2 + s, b, c2

    def sync(self, sp, side=None):
        t = self.t
        for dst, src in ((self.nullv, t["null_v_row"]), (self.late, t["late"]), (self.ident, t["ident"])):
            sp.dma_start(dst[:, :], src).then_inc(self.const_in, 16)

        def load(g):
            s, b, c = g % 2, self.b0 + g // DC, g % DC
            if g >= 2:
                sp.wait_ge(self.pv_done, (g - 1) * UNITS + 2)
            sp.dma_start(self.q[s][:, :], t["q"][c, :, b * SEQ:(b + 1) * SEQ]).then_inc(self.item_in[s], 16)
            sp.dma_start(self.kc[s][:, :], t["kc"][c, :, b * NC:(b + 1) * NC]).then_inc(self.item_in[s], 16)
            sp.dma_start(self.vc[s][:, :, :],
                         t["vc"][b * NC:(b + 1) * NC, c * P:(c + 1) * P].rearrange("(n p) d -> p n d", p=P))\
                .then_inc(self.item_in[s], 16)
            sp.dma_start(self.nk[s][:, :], t["null_bd"][c, :, :]).then_inc(self.item_in[s], 16)

        load(0)
        load(1)
        for g in range(self.items):
            if side:
                side(g)
            if g + 2 < self.items:
                load(g + 2)
            sp.wait_ge(self.raw_ready, g + 1)
            b, c = self.b0 + g // DC, g % DC
            sp.dma_start(t["att"][b * SEQ:(b + 1) * SEQ, c * P:(c + 1) * P].rearrange("(i p) d -> p i d", p=P),
                         self.raw[g % 2][:, :, :]).then_inc(self.att_out[g % 2], 16)
        for s in range(2):
            sp.wait_ge(self.att_out[s], 16 * (self.items // 2 + 1))

    def tensor(self, pe):
        pe.wait_ge(self.const_in, 16 * 3)
        pe.wait_ge(self.zeroed, 1)
        pe.sem_inc(self.p_transposed, 2)
        pe.sem_inc(self.pv_done, 2)
        for s, g, b, c2 in self.each_item(pe):
            pe.wait_ge(self.item_in[s], (b * (DC // 2) + c2 + 1) * 64)
            o = self.ps_o[s % 2]
            pe.wait_ge(self.o_emptied, g * QT + 1)
            for i in range(QT):
                last = pe.matmul(o[:, i * HPC:(i + 1) * HPC], self.q[s][:, i * P:(i + 1) * P], self.nk[s][:, :],
                                 start=True, stop=True)
            last.then_inc(self.s0_filled, 1)
            for m in range(UNITS + 2):
                if m < UNITS:
                    i, w = m // PAIRS, KW * (m // PAIRS + 1)
                    pe.wait_ge(self.s_emptied, g * UNITS + m + 1)
                    for h in range(2):
                        rows = slice((m % PAIRS * 2 + h) * DH, (m % PAIRS * 2 + h + 1) * DH)
                        last = pe.matmul(self.ps_s[m % 2][:, h, 0:w], self.q[s][rows, i * P:(i + 1) * P],
                                         self.kc[s][rows, 0:w], start=True, stop=True)
                    last.then_inc(self.s_filled, 1)
                if 1 <= m <= UNITS:
                    u = m - 1
                    w = KW * (u // PAIRS + 1)
                    pe.wait_ge(self.s_emptied, g * UNITS + u + 3)
                    pe.wait_ge(self.t0_emptied, g * UNITS + u + 1)
                    hold(pe, self.t1_emptied, g * UNITS + u + 1, self.passed)
                    for h in range(2):
                        for k0 in range(0, w, P):
                            kw = min(P, w - k0)
                            last = pe.transpose(self.ps_t[h][0:kw, k0:k0 + P], self.p[u % 2][:, h, k0:k0 + kw],
                                                self.ident[:, :])
                    last.then_inc(self.p_transposed, 1)
                if m >= 2:
                    u = m - 2
                    i, w = u // PAIRS, KW * (u // PAIRS + 1)
                    pe.wait_ge(self.t0_emptied, g * UNITS + u + 2)
                    pe.wait_ge(self.t1_emptied, g * UNITS + u + 2)
                    o = self.ps_o[(s + i + 1) % 2]
                    if u % PAIRS == 0 and i == 1:
                        pe.wait_ge(self.s0_emptied, g + 1)
                    elif u % PAIRS == 0:
                        pe.wait_ge(self.o_emptied, g * QT + (2 if i == 0 else i + 1))
                    for h in range(2):
                        head = u % PAIRS * 2 + h
                        for k0 in range(0, w, P):
                            kw = min(P, w - k0)
                            last = pe.matmul(o[:, head * DH:(head + 1) * DH], self.pT[u % 2][0:kw, h, k0:k0 + P],
                                             self.vc[s][0:kw, k0 // P, head * DH:(head + 1) * DH], start=k0 == 0,
                                             stop=k0 + P >= w)
                    last.then_inc(self.pv_done, 1)

    def pT_out(self, eng, copy, h, g, u, emptied):
        w = KW * (u // PAIRS + 1)
        n = -(-w // P) * P
        eng.wait_ge(self.p_transposed, g * UNITS + u + 3)
        eng.wait_ge(self.pv_done, g * UNITS + u + 1)
        copy(self.pT[u % 2][:, h, 0:n], self.ps_t[h][:, 0:n]).then_inc(emptied, 1)

    def scalar(self, act):
        act.sem_inc(self.s_emptied, 2)
        act.sem_inc(self.t1_emptied, 1)
        act.sem_inc(self.o_emptied, 2)
        for s, g, b, c2 in self.each_item(act):
            for m in range(UNITS + 2):
                if m < UNITS:
                    i, w, h0 = m // PAIRS, KW * (m // PAIRS + 1), m % PAIRS * 2
                    act.wait_ge(self.nm_ready, g * UNITS + m + 1)
                    act.wait_ge(self.p_transposed, g * UNITS + m + 1)
                    for h in range(2):
                        last = act.activation(self.p[m % 2][:, h, 0:w], self.ps_s[m % 2][:, h, 0:w], ACT.Exp,
                                              bias=self.nm[s][:, i, h0 + h:h0 + h + 1], scale=SCALE,
                                              accum_out=self.rs[s][:, i, h0 + h:h0 + h + 1])
                    last.then_inc(self.s_emptied, 1)
                if 1 <= m <= UNITS:
                    self.pT_out(act, act.copy, 1, g, m - 1, self.t1_emptied)
                if m >= 3 and m % PAIRS == 1:
                    i = (m - 3) // PAIRS
                    if i == 0:
                        act.wait_ge(self.att_out[s], (b * (DC // 2) + c2 + 1) * 16)
                    act.wait_ge(self.pv_done, g * UNITS + 2 * i + 4)
                    act.copy(self.raw[s][:, i, :], self.ps_o[(s + i + 1) % 2][:, 0:P]).then_inc(self.o_emptied, 1)
            act.wait_ge(self.d0_ready, g + 1)
            act.activation(self.p0[:, :, :], self.d0[:, :, :], ACT.Exp).then_inc(self.p0_ready, 1)

    MARKS = 2 * UNITS + 4

    def vector(self, dve, side):
        for h in range(2):
            last = dve.memset(self.ps_t[h][:, :], 0.0)
        last.then_inc(self.zeroed, 1)
        dve.wait_ge(self.const_in, 16 * 3)
        dve.sem_inc(self.t0_emptied, 1)
        dve.sem_inc(self.att_out[0], 16)
        dve.sem_inc(self.att_out[1], 16)
        for s, g, b, c2 in self.each_item(dve):
            st = Steps(dve, self.dve_done, g * self.MARKS)
            dve.wait_ge(self.s0_filled, g + 1)
            dve.tensor_scalar(self.s0n[s][:, :, :].rearrange("p i h -> p (i h)"), self.ps_o[s % 2][:, 0:QT * HPC], -SCALE,
                              None, ALU.mult).then_inc(self.s0_emptied, 1)
            dve.wait_ge(self.s0_emptied, g + 1)
            for m in range(UNITS + 1):
                if m < UNITS:
                    i, w, h0 = m // PAIRS, KW * (m // PAIRS + 1), m % PAIRS * 2
                    S = self.ps_s[m % 2]
                    dve.wait_ge(self.s_filled, g * UNITS + m + 1)
                    st.mark(dve.tensor_tensor(S[:, :, w - KW:w], S[:, :, w - KW:w],
                                              self.late[:, None, :].broadcast_to([P, 2, KW]), ALU.add))
                    st.wait()
                    st.mark(dve.tensor_reduce(self.mx[:, m % 2, :], S[:, :, 0:w], AX, ALU.max))
                    st.wait()
                    dve.scalar_tensor_tensor(self.nm[s][:, i, h0:h0 + 2], self.mx[:, m % 2, :], -SCALE,
                                             self.s0n[s][:, i, h0:h0 + 2], ALU.mult, ALU.min)\
                        .then_inc(self.nm_ready, 1)
                if m >= 1:
                    self.pT_out(dve, dve.tensor_copy, 0, g, m - 1, self.t0_emptied)
                if m % PAIRS == 1:
                    side(g, m // PAIRS)
            dve.wait_ge(self.nm_ready, (g + 1) * UNITS)
            dve.tensor_tensor(self.d0[:, :, :], self.nm[s][:, :, :], self.s0n[s][:, :, :], ALU.subtract)\
                .then_inc(self.d0_ready, 1)
            dve.wait_ge(self.p0_ready, g + 1)
            st.mark(dve.tensor_tensor(self.den[:, :, :], self.rs[s][:, :, :], self.p0[:, :, :], ALU.add))
            bc = c2 * 2 + s

            def flat(a):
                return a[:, :, :].rearrange("p i h -> p (i h)")

            st.mark(dve.tensor_tensor(
                self.nulls[:, :, :].rearrange("p i (h d) -> p i h d", h=HPC),
                self.nullv[:, bass.ds(bc * P, P)].rearrange("p (a h d) -> p a h d", a=1, h=HPC).broadcast_to([P, QT, HPC, DH]),
                self.p0[:, :, :, None].broadcast_to([P, QT, HPC, DH]), ALU.mult))
            st.wait()
            st.mark(dve.reciprocal(flat(self.rden), flat(self.den)))
            dve.wait_ge(self.o_emptied, (g + 1) * QT + 2)
            st.mark(dve.tensor_tensor(self.raw[s][:, :, :], self.raw[s][:, :, :], self.nulls[:, :, :], ALU.add))
            st.wait()
            r4 = self.raw[s][:, :, :].rearrange("p i (h d) -> p (i h) d", h=HPC)
            dve.tensor_tensor(r4, r4, flat(self.rden)[:, :, None].broadcast_to([P, QT * HPC, DH]), ALU.mult)\
                .then_inc(self.raw_ready, 1)
            assert st.n == self.MARKS, st.n



def stage_b(nc, t):
    ctx = ExitStack()
    with ctx:
        sb, ps, sem = opener(nc, ctx)
        att = Attention(nc, ctx, t, 0, BATCH // 2, "b_")
        NE = NTILE * EXPERTS
        pos = sb("s_pos", [P, NTILE, EXPERTS])
        w = sb("s_w", [P, NTILE, EXPERTS])
        slot = sb("s_slot", [P, NTILE, EXPERTS])
        tmp = sb("s_tmp", [P, NTILE, EXPERTS])
        cnt = sb("s_cnt", [P, EXPERTS])
        cnti = sb("s_cnti", [P, EXPERTS], I32)
        nbf = sb("s_nbf", [P, EXPERTS])
        incl = sb("s_incl", [P, EXPERTS])
        start = sb("s_start", [P, EXPERTS])
        onesf = sb("s_onesf", [P, EXPERTS])
        bidx = sb("s_bidx", [P, 3])
        bcmp = sb("s_bcmp", [P, 3, EXPERTS])
        bexp = sb("s_bexp", [P, 3])
        bexpi = sb("s_bexpi", [P, 3], I32)
        s8 = sb("s_s8", [P, NTILE, TOPK])
        s8i = sb("s_s8i", [P, NTILE, TOPK], I32)
        lo = sb("s_lo", [P, NTILE * TOPK], I32)
        cell = sb("s_cell", [P, NTILE * TOPK], I32)
        w8 = sb("s_w8", [P, NTILE, TOPK])
        tokens = sb("s_tokens", [P, NTILE], I32)
        zeros = sb("s_zeros", [P, NCOL], I32)
        ix = [sb(f"s_ix{r}", [P, TOPK], I32) for r in range(2)]
        tk = [sb(f"s_tk{r}", [P, 1], I32) for r in range(2)]

        passed = sem("s_passed")
        tab_in = sem("s_tab_in")
        done = sem("s_done")
        w8_done = sem("s_w8_done")
        zero_ready = sem("s_zero_ready")
        ids_zeroed = sem("s_ids_zeroed")
        blk_ready = sem("s_blk_ready")
        cell_ready = sem("s_cell_ready")
        w8_ready = sem("s_w8_ready")
        out = sem("s_out")
        ix_ready = sem("s_ix_ready")
        scattered = [sem(f"s_scattered{r}") for r in range(2)]
        block = ctx.enter_context(nc.Block())

        @block.sync
        def _(sp):
            sp.dma_start(cnt[:, :], t["cnt"]).then_inc(tab_in, 16)
            sp.dma_start(bidx[:, :], t["bidx"]).then_inc(tab_in, 16)
            sp.dma_start(pos[:, :, :].rearrange("p a e -> p (a e)"), t["pos"]).then_inc(tab_in, 16)
            sp.dma_start(w[:, :, :].rearrange("p a e -> p (a e)"), t["w"]).then_inc(tab_in, 16)
            sp.wait_ge(zero_ready, 1)
            sp.dma_start(t["ids"].rearrange("(p n) a -> p (n a)", p=P), zeros[:, :]).then_inc(ids_zeroed, 16)
            att.sync(sp)
            sp.wait_ge(blk_ready, 1)
            sp.dma_start(t["blk"].rearrange("a (p j) -> (a p) j", p=P), bexpi[:, :]).then_inc(out, 16)
            sp.wait_ge(cell_ready, 1)
            sp.dma_start(t["slot8"], s8i[:, :, :].rearrange("p a k -> p (a k)")).then_inc(out, 16)
            sp.wait_ge(w8_ready, TOPK)
            sp.dma_start(t["w8"], w8[:, :, :].rearrange("p a k -> p (a k)")).then_inc(out, 16)
            sp.wait_ge(out, 48)

        @block.gpsimd
        def _(pool):
            pool.memset(zeros[:, :], 0).then_inc(zero_ready, 1)
            pool.iota(tokens[:, :], pattern=[[P, NTILE]], base=0, channel_multiplier=1).then_inc(ix_ready, 1)
            pool.wait_ge(ids_zeroed, 16)
            pool.wait_ge(cell_ready, 1)
            hold(pool, ix_ready, 1, passed)

            def scatter(i, r, first):
                n = i * 2 + r
                if not first:
                    hold(pool, scattered[r], i * 16 * TOPK, passed)
                pool.tensor_copy(ix[r][:, :], cell[:, bass.ds(n * TOPK, TOPK)]).then_inc(ix_ready, 1)
                pool.tensor_copy(tk[r][:, :], tokens[:, bass.ds(n, 1)]).then_inc(ix_ready, 1)
                hold(pool, ix_ready, n * 2 + 3, passed)
                for k in range(TOPK):
                    pool.indirect_dma_start(t["ids"], bass.IndirectOffsetOnAxis(ap=ix[r][:, k:k + 1], axis=0), tk[r][:, :],
                                            None).then_inc(scattered[r], 16)

            for r in range(2):
                scatter(0, r, True)
            with pool.Fori(1, NTILE // 2) as i:
                for r in range(2):
                    scatter(i, r, False)
            for r in range(2):
                pool.wait_ge(scattered[r], NTILE // 2 * 16 * TOPK)

        @block.scalar
        def _(act):
            att.scalar(act)

        @block.tensor
        def _(pe):
            att.tensor(pe)

        @block.vector
        def _(dve):
            st = Steps(dve, done, 0)

            def do(instruction):
                st.mark(instruction)
                st.wait()

            dve.wait_ge(tab_in, 64)
            do(dve.memset(onesf[:, :], 1.0))
            do(dve.tensor_scalar(cnti[:, :], cnt[:, :], float(RB - 1), None, ALU.add))
            do(dve.tensor_scalar(cnti[:, :], cnti[:, :], RB.bit_length() - 1, None, ALU.logical_shift_right))
            do(dve.tensor_copy(nbf[:, :], cnti[:, :]))
            do(dve.tensor_tensor_scan(incl[:, :], onesf[:, :], nbf[:, :], 0.0, ALU.mult, ALU.add))
            do(dve.tensor_tensor(start[:, :], incl[:, :], nbf[:, :], ALU.subtract))
            do(dve.tensor_scalar(start[:, :], start[:, :], float(RB), None, ALU.mult))
            do(dve.tensor_tensor(bcmp[:, :, :], incl[:, None, :].broadcast_to([P, 3, EXPERTS]),
                                 bidx[:, :, None].broadcast_to([P, 3, EXPERTS]), ALU.is_le))
            do(dve.tensor_reduce(bexp[:, :], bcmp[:, :, :], AX, ALU.add))
            st.mark(dve.tensor_scalar(bexpi[:, :], bexp[:, :], float(EXPERTS - 1), None, ALU.min))
            st.wait()
            dve.sem_inc(blk_ready, 1)
            do(dve.scalar_tensor_tensor(slot[:, :, :], pos[:, :, :], 0.0,
                                        start[:, None, :].broadcast_to([P, NTILE, EXPERTS]), ALU.is_gt, ALU.mult))
            do(dve.tensor_tensor(slot[:, :, :], slot[:, :, :], pos[:, :, :], ALU.add))
            for n in range(NTILE):
                st.mark(dve.max(s8[:, n, :], slot[:, n, :]))
            st.wait()
            do(dve.tensor_scalar(s8i[:, :, :], s8[:, :, :], -1.0, None, ALU.add))
            s8f = s8i[:, :, :].rearrange("p a k -> p (a k)")
            do(dve.tensor_scalar(lo[:, :], s8f, P - 1, None, ALU.bitwise_and))
            do(dve.tensor_scalar(cell[:, :], s8f, P.bit_length() - 1, None, ALU.logical_shift_right))
            do(dve.scalar_tensor_tensor(cell[:, :], lo[:, :], float(NCOL), cell[:, :], ALU.mult, ALU.add))
            dve.sem_inc(cell_ready, 1)

            def weights(g, i):
                if i in (2, 6, 10):
                    shape = [P, NTILE, EXPERTS]
                    ws = Steps(dve, w8_done, g * 2)
                    if i == 2:
                        ws.mark(dve.tensor_tensor(tmp[:, :, :], slot[:, :, :], s8[:, :, bass.ds(g, 1)].broadcast_to(shape),
                                                  ALU.is_equal))
                    elif i == 6:
                        ws.n = 1
                        ws.wait()
                        ws.mark(dve.tensor_tensor(tmp[:, :, :], tmp[:, :, :], w[:, :, :], ALU.mult))
                    else:
                        ws.n = 2
                        ws.wait()
                        dve.tensor_reduce(w8[:, :, bass.ds(g, 1)], tmp[:, :, :], AX, ALU.add).then_inc(w8_ready, 1)

            att.vector(dve, weights)



def stage_e(nc, t):
    ctx = ExitStack()
    with ctx:
        sb, ps, sem = opener(nc, ctx, "e_")
        HC = HID // P
        ident = sb("ident", [P, P])
        blk = sb("blk", [1, 3 * P], I32)
        ids = sb("ids", [P, NCOL], I32)
        ix = [sb(f"ix{s}", [P, RT], I32) for s in range(2)]
        xg = [sb(f"xg{s}", [P, RT, DIM]) for s in range(2)]
        xT = sb("xT", [P, DC, RB])
        wg = [sb(f"wg{s}", [P, DC, HID]) for s in range(2)]
        wu = [sb(f"wu{s}", [P, DC, HID]) for s in range(2)]
        wd = [sb(f"wd{s}", [P, HC, DIM]) for s in range(2)]
        sg = [sb(f"sg{s}", [P, HC * RB]) for s in range(2)]
        gated = [sb(f"gated{s}", [P, HC * RB]) for s in range(2)]
        hT = [sb(f"hT{s}", [P, HC * RB]) for s in range(2)]
        rows = [sb(f"rows{s}", [P, RT, DIM]) for s in range(2)]
        ps_t = [ps(f"ps_t{i}", [P, DC // 2 * RB]) for i in range(2)]
        ps_g = [ps(f"ps_g{s}", [P, HC * RB]) for s in range(2)]
        ps_u = [ps(f"ps_u{s}", [P, HC * RB]) for s in range(2)]
        ps_y = [ps(f"ps_y{i}", [P, DIM]) for i in range(RT)]

        passed = sem("passed")
        const_in = sem("const_in")
        gathered = [sem(f"gathered{s}") for s in range(2)]
        gu_in = [sem(f"gu_in{s}") for s in range(2)]
        d_in = [sem(f"d_in{s}") for s in range(2)]
        ix_ready = sem("ix_ready")
        t_filled = sem("t_filled")
        t0_emptied = sem("t0_emptied")
        t1_emptied = sem("t1_emptied")
        g_filled = sem("g_filled")
        u_filled = sem("u_filled")
        sig_ready = sem("sig_ready")
        g_emptied = sem("g_emptied")
        h_ready = sem("h_ready")
        y_filled = sem("y_filled")
        y_emptied = sem("y_emptied")
        rows_out = [sem(f"rows_out{s}") for s in range(2)]

        def turn(b):
            return b // 2 + 1

        def blocks(eng, first, step):
            assert (NBLK - 1 - first) % 2 == 0
            with eng.Fori(0, (NBLK - 1 - first) // 2) as i:
                for r in range(2):
                    step(i * 2 + first + r, (first + r) % 2, i + (first + r) // 2)

        block = ctx.enter_context(nc.Block())

        @block.sync
        def _(sp):
            sp.dma_start(blk[:, :], t["blk"]).then_inc(const_in, 16)
            sp.dma_start(ident[:, :], t["ident"]).then_inc(const_in, 16)
            sp.dma_start(ids[:, :], t["ids"].rearrange("(p n) a -> p (n a)", p=P)).then_inc(const_in, 16)
            sp.wait_ge(const_in, 48)

            def load_gu(b, s, first):
                if not first:
                    hold(sp, u_filled, b - 1, passed)
                e = sp.value_load(blk[0:1, bass.ds(b, 1)], min_val=0, max_val=EXPERTS - 1)
                for dst, src in ((wg, t["gate_w"]), (wu, t["up_w"])):
                    sp.dma_start(dst[s][:, :, :], src[bass.ds(e, 1), :, :].rearrange("a (k p) h -> p (a k) h", p=P))\
                        .then_inc(gu_in[s], 16)
                return e

            def load_d(e, b, s, first):
                if not first:
                    hold(sp, y_filled, b * 2 + 2, passed)
                sp.dma_start(wd[s][:, :, :], t["down_w"][bass.ds(e, 1), :, :].rearrange("a (k p) c -> p (a k) c", p=P))\
                    .then_inc(d_in[s], 16)

            def store(b, s):
                hold(sp, y_emptied, b * 2 + 4, passed)
                sp.dma_start(t["rows"][bass.ds(b * RB, RB), :].rearrange("(i p) c -> p i c", p=P), rows[s][:, :, :])\
                    .then_inc(rows_out[s], 16)

            for b in range(2):
                load_d(load_gu(b, b, True), b, b, True)

            def step(b, s, i):
                e = load_gu(b + 1, 1 - s, False)
                load_d(e, b + 1, 1 - s, False)
                store(b - 1, 1 - s)

            blocks(sp, 1, step)
            store(NBLK - 2, NBLK % 2)
            store(NBLK - 1, 1 - NBLK % 2)
            for s in range(2):
                sp.wait_ge(rows_out[s], 16 * (NBLK // 2 + 1))

        @block.gpsimd
        def _(pool):
            hold(pool, const_in, 48, passed)

            def gather(b, s, first):
                if not first:
                    hold(pool, t_filled, b * 2 - 2, passed)
                pool.tensor_copy(ix[s][:, :], ids[:, bass.ds(b * RT, RT)]).then_inc(ix_ready, 1)
                hold(pool, ix_ready, b + 1, passed)
                for i in range(RT):
                    pool.indirect_dma_start(xg[s][:, i, :], None, t["xn"],
                                            bass.IndirectOffsetOnAxis(ap=ix[s][:, i:i + 1], axis=0))\
                        .then_inc(gathered[s], 16)

            gather(0, 0, True)
            gather(1, 1, True)
            with pool.Fori(1, NBLK // 2) as i:
                for s in range(2):
                    gather(i * 2 + s, s, False)

        @block.scalar
        def _(act):
            act.sem_inc(y_emptied, 2)

            def xT_out(b):
                act.wait_ge(t_filled, b * 2 + 2)
                act.copy(xT[:, DC // 2:DC, :].rearrange("p k n -> p (k n)"), ps_t[1][:, :]).then_inc(t1_emptied, 1)

            def sigmoid(b, s):
                act.wait_ge(g_filled, b + 1)
                act.wait_ge(g_emptied, b + 1)
                act.activation(sg[s][:, :], ps_g[s][:, :], ACT.Sigmoid).then_inc(sig_ready, 1)

            def y_out(b, s, turn_):
                act.wait_ge(rows_out[s], (turn_ + 1) * 16)
                for i in range(RT):
                    act.wait_ge(y_filled, b * 2 + i + 5)
                    act.copy(rows[s][:, i, :], ps_y[i][:, :]).then_inc(y_emptied, 1)

            xT_out(0)
            sigmoid(0, 0)
            xT_out(1)

            def step(b, s, i):
                sigmoid(b, s)
                xT_out(b + 1)
                y_out(b - 1, 1 - s, i if s else i - 1)

            blocks(act, 1, step)
            b = NBLK - 1
            sigmoid(b, b % 2)
            y_out(b - 1, (b - 1) % 2, (b - 1) // 2)
            y_out(b, b % 2, b // 2)

        @block.vector
        def _(dve):
            dve.sem_inc(g_emptied, 2)
            dve.sem_inc(h_ready, 2)
            for s in range(2):
                dve.sem_inc(rows_out[s], 16)

            def xT_out(b):
                dve.wait_ge(t_filled, b * 2 + 1)
                dve.tensor_copy(xT[:, 0:DC // 2, :].rearrange("p k n -> p (k n)"), ps_t[0][:, :]).then_inc(t0_emptied, 1)

            def hidden(b, s):
                dve.wait_ge(sig_ready, b + 1)
                dve.tensor_tensor(gated[s][:, :], sg[s][:, :], ps_g[s][:, :], ALU.mult).then_inc(g_emptied, 1)
                dve.wait_ge(u_filled, b + 1)
                dve.wait_ge(g_emptied, b + 3)
                dve.wait_ge(y_filled, b * 2 + 2)
                dve.tensor_tensor(hT[s][:, :], gated[s][:, :], ps_u[s][:, :], ALU.mult).then_inc(h_ready, 1)

            xT_out(0)
            hidden(0, 0)
            xT_out(1)

            def step(b, s, i):
                hidden(b, s)
                xT_out(b + 1)

            blocks(dve, 1, step)
            hidden(NBLK - 1, (NBLK - 1) % 2)

        @block.tensor
        def _(pe):
            pe.sem_inc(y_filled, 4)
            pe.wait_ge(const_in, 48)

            def transposes(b, s, turn_):
                hold(pe, gathered[s], (turn_ + 1) * 16 * RT, passed)
                for k in range(DC):
                    for i in range(RT):
                        o = k % 2 * RB + i * P
                        last = pe.transpose(ps_t[k // 2][:, o:o + P], xg[s][:, i, k * P:(k + 1) * P], ident[:, :])
                    if k % 2:
                        last.then_inc(t_filled, 1)

            def gate_up(b, s, turn_):
                pe.wait_ge(gu_in[s], (turn_ + 1) * 32)
                pe.wait_ge(t0_emptied, b + 1)
                pe.wait_ge(t1_emptied, b + 1)
                for wt, dst, free, filled in ((wg, ps_g, g_emptied, g_filled), (wu, ps_u, h_ready, u_filled)):
                    pe.wait_ge(free, b + 1)
                    for h in range(HC):
                        for k in range(DC):
                            last = pe.matmul(dst[s][:, h * RB:(h + 1) * RB], wt[s][:, k, h * P:(h + 1) * P], xT[:, k, :],
                                             start=k == 0, stop=k == DC - 1)
                    last.then_inc(filled, 1)

            def down(b, s, turn_):
                pe.wait_ge(d_in[s], (turn_ + 1) * 16)
                pe.wait_ge(h_ready, b + 3)
                for i in range(RT):
                    pe.wait_ge(y_emptied, b * 2 + i + 1)
                    for h in range(HC):
                        last = pe.matmul(ps_y[i][:, :], hT[s][:, h * RB + i * P:h * RB + (i + 1) * P], wd[s][:, h, :],
                                         start=h == 0, stop=h == HC - 1)
                    last.then_inc(y_filled, 1)

            transposes(0, 0, 0)
            gate_up(0, 0, 0)
            transposes(1, 1, 0)

            def step(b, s, i):
                gate_up(b, s, i)
                transposes(b + 1, 1 - s, i + s)
                down(b - 1, 1 - s, i if s else i - 1)

            blocks(pe, 1, step)
            b = NBLK - 1
            gate_up(b, b % 2, b // 2)
            down(b - 1, (b - 1) % 2, (b - 1) // 2)
            down(b, b % 2, b // 2)



def stage_f(nc, t):
    ctx = ExitStack()
    with ctx:
        sb, ps, sem = opener(nc, ctx, "f_")
        att = Attention(nc, ctx, t, BATCH // 2, BATCH // 2, "g_")
        TPI = NTILE // att.items
        slots = sb("slots", [P, NTILE * TOPK], I32)
        w8 = sb("w8", [P, NTILE * TOPK])
        ix = [sb(f"ix{r}", [P, TOPK], I32) for r in range(2)]
        xs = [sb(f"xs{r}", [P, 2, DIM]) for r in range(2)]
        got = [sb(f"got{r}", [P, TOPK, DIM]) for r in range(2)]
        acc = [sb(f"acc{r}", [P, DIM]) for r in range(2)]

        passed = sem("passed")
        tab_in = sem("tab_in")
        xs_in = [sem(f"xs_in{r}") for r in range(2)]
        ix_ready = sem("ix_ready")
        gathered = [sem(f"gathered{r}") for r in range(2)]
        step_done = sem("step_done")
        acc_ready = sem("acc_ready")
        base_out = [sem(f"base_out{r}") for r in range(2)]
        block = ctx.enter_context(nc.Block())

        @block.sync
        def _(sp):
            sp.dma_start(slots[:, :], t["slot8"]).then_inc(tab_in, 16)
            sp.dma_start(w8[:, :], t["w8"]).then_inc(tab_in, 16)

            def load(n, r):
                sp.dma_start(xs[r][:, 0, :], t["x"][bass.ds(n * P, P), :]).then_inc(xs_in[r], 16)
                sp.dma_start(xs[r][:, 1, :], t["shared"][bass.ds(n * P, P), :]).then_inc(xs_in[r], 16)

            def tiles(g):
                def one(n, r, load_too):
                    hold(sp, acc_ready, n + 1, passed)
                    if load_too:
                        load(n + 2, r)
                    sp.dma_start(t["base"][bass.ds(n * P, P), :], acc[r][:, :]).then_inc(base_out[r], 16)

                full = g < att.items - 1
                with sp.Fori(0, TPI // 2 - (0 if full else 1)) as i:
                    for r in range(2):
                        one(i * 2 + g * TPI + r, r, True)
                if not full:
                    for r in range(2):
                        one(NTILE - 2 + r, r, False)

            load(0, 0)
            load(1, 1)
            att.sync(sp, tiles)
            for r in range(2):
                sp.wait_ge(base_out[r], 16 * (NTILE // 2 + 1))

        @block.gpsimd
        def _(pool):
            hold(pool, tab_in, 32, passed)

            def gather(i, r, first):
                n = i * 2 + r
                if not first:
                    hold(pool, acc_ready, n - 1, passed)
                pool.tensor_copy(ix[r][:, :], slots[:, bass.ds(n * TOPK, TOPK)]).then_inc(ix_ready, 1)
                hold(pool, ix_ready, n + 1, passed)
                for k in range(TOPK):
                    pool.indirect_dma_start(got[r][:, k, :], None, t["rows"],
                                            bass.IndirectOffsetOnAxis(ap=ix[r][:, k:k + 1], axis=0))\
                        .then_inc(gathered[r], 16)

            for r in range(2):
                gather(0, r, True)
            with pool.Fori(1, NTILE // 2) as i:
                for r in range(2):
                    gather(i, r, False)

        @block.scalar
        def _(act):
            att.scalar(act)

        @block.tensor
        def _(pe):
            att.tensor(pe)

        @block.vector
        def _(dve):
            for r in range(2):
                dve.sem_inc(base_out[r], 16)
            dve.wait_ge(tab_in, 32)

            def combine(g, i):
                if i % 2 == 0:
                    return
                f, r = i // 2, i // 2 % 2
                n = g * TPI + f
                turn_ = g * (TPI // 2) + f // 2
                st = Steps(dve, step_done, n * TOPK)
                dve.wait_ge(xs_in[r], turn_ * 32 + 32)
                dve.wait_ge(base_out[r], turn_ * 16 + 16)
                st.mark(dve.tensor_tensor(acc[r][:, :], xs[r][:, 0, :], xs[r][:, 1, :], ALU.add))
                dve.wait_ge(gathered[r], turn_ * (16 * TOPK) + 16 * TOPK)
                for k in range(TOPK):
                    st.wait()
                    last = dve.scalar_tensor_tensor(acc[r][:, :], got[r][:, k, :], w8[:, bass.ds(n * TOPK + k, 1)],
                                                    acc[r][:, :], ALU.mult, ALU.add)
                    if k < TOPK - 1:
                        st.mark(last)
                last.then_inc(acc_ready, 1)

            att.vector(dve, combine)



def stage_c(nc, t):
    ctx = ExitStack()
    with ctx:
        sb, ps, sem = opener(nc, ctx, "c_")
        HT = SEQ // 2 // P
        NP = BATCH * HT
        NCOS, NSIN = DIM // 2 + 1, DIM // 2 - 1
        MB = SEQ // 4 // P
        wout = sb("wout", [P, DC, DIM])
        dft = sb("dft", [P, DC, DIM])
        w2 = sb("w2", [P, DC, DIM])
        bcol = sb("bcol", [P, DC])
        brep = sb("brep", [P, DC, P])
        b2 = sb("b2", [P, DIM])
        ident = sb("ident", [P, P])
        alt = sb("alt", [P, 1])
        att = sb("att", [P, 2, DIM])
        sd = [sb(f"sd{v}", [P, DIM]) for v in range(2)]
        sdT = [sb(f"sdT{v}", [P, DC, P]) for v in range(2)]
        y = [sb(f"y{v}", [P, NP, DIM]) for v in range(2)]
        qs = [sb(f"qs{r}", [P, NCOS]) for r in range(2)]
        dif = [sb(f"dif{r}", [P, NCOS]) for r in range(2)]
        turned = [sb(f"turned{r}", [P, DIM]) for r in range(2)]
        flip = sb("flip", [P, P])
        base = [[sb(f"base{v}{r}", [P, DIM]) for r in range(2)] for v in range(2)]
        ps_t = [ps(f"ps_t{v}", [P, DIM]) for v in range(2)]
        ps_y = [ps(f"ps_y{v}", [P, DIM]) for v in range(2)]
        ps_p = [ps(f"ps_p{r}", [P, 512]) for r in range(2)]
        ps_q = [ps(f"ps_q{r}", [P, 512]) for r in range(2)]
        cos = [wout, dft]
        sin = [sb(f"sin{v}", [P, HT, P]) for v in range(2)]
        cos = [c[:, :, :].rearrange("p k n -> p (k n)")[:, 0:HT * P].rearrange("p (k n) -> p k n", k=HT) for c in cos]

        passed = sem("passed")
        const_in = sem("const_in")
        brep_ready = sem("brep_ready")
        att_in = sem("att_in")
        sd_ready = sem("sd_ready")
        w_filled = sem("w_filled")
        w_emptied = sem("w_emptied")
        t_filled = sem("t_filled")
        t_emptied = sem("t_emptied")
        y_filled = sem("y_filled")
        y_emptied = sem("y_emptied")
        tab_in = [sem(f"tab_in{v}") for v in range(2)]
        p_filled = sem("p_filled")
        q_filled = sem("q_filled")
        p_emptied = sem("p_emptied")
        q_emptied = sem("q_emptied")
        dve_done = sem("dve_done")
        qs_zeroed = sem("qs_zeroed")
        base_in = [sem(f"base_in{r}") for r in range(2)]
        turned_ready = sem("turned_ready")
        r_filled = sem("r_filled")
        out_ready = sem("out_ready")
        out_done = [sem(f"out_done{r}") for r in range(2)]
        last_in = sem("last_in")
        last_filled = sem("last_filled")
        last_ready = sem("last_ready")
        last_done = sem("last_done")
        block = ctx.enter_context(nc.Block())

        U = 2 * BATCH
        NU = MB * U

        @block.sync
        def _(sp):
            for dst, src in ((wout, t["wout_t"]), (dft, t["dft_d"])):
                sp.dma_start(dst[:, :, :], src.rearrange("(k p) n -> p k n", p=P)).then_inc(const_in, 16)
            for dst, src in ((bcol, t["b_out_col"]), (ident, t["ident"]), (alt, t["alt"]), (flip, t["flip"])):
                sp.dma_start(dst[:, :], src).then_inc(const_in, 16)
            with sp.Fori(0, BATCH) as b:
                with sp.Fori(0, HT) as i:
                    hold(sp, sd_ready, (b * HT + i) * 2 + 2, passed)
                    for v in range(2):
                        sp.dma_start(att[:, v, :], t["att"][bass.ds(b * SEQ + i * P + v * HT * P, P), :]).then_inc(att_in, 16)

            def unit(n):
                m, v, b = n // U, n // BATCH % 2, n % BATCH
                k1 = [b * SEQ + (m * P + p) * 2 + v for p in (0, P - 1)]
                rows = P - 1 if (m, v) == (0, 0) else P
                up = t["base"][k1[0]:k1[1] + 1:2, :], t["out"][k1[0]:k1[1] + 1:2, :]
                lo = (2 * b + 1) * SEQ - k1[1]
                down = [a[lo:lo + 2 * rows - 1:2, :] for a in (t["base"], t["out"])]
                return rows, up, down

            def load_base(n):
                r = n % 2
                rows, up, down = unit(n)
                if n >= 2:
                    sp.wait_ge(out_done[r], 32 * (n // 2))
                sp.dma_start(base[0][r][:, :], up[0]).then_inc(base_in[r], 16)
                sp.dma_start(base[1][r][0:rows, :], down[0]).then_inc(base_in[r], 16)

            def load_tables(m, v):
                if (m, v) == (0, 0):
                    sp.wait_ge(w_filled, DC + 1)
                if m:
                    sp.wait_ge(q_filled, (m - 1) * U + (v + 1) * BATCH)
                sp.dma_start(cos[v], t["cos_t"][v, m, :, :, :]).then_inc(tab_in[v], 16)
                sp.dma_start(sin[v][:, :, :], t["sin_t"][v, m, :, :, :]).then_inc(tab_in[v], 16)

            for v in range(2):
                load_tables(0, v)
            sp.wait_ge(qs_zeroed, 1)
            load_base(0)
            load_base(1)
            for n in range(NU):
                sp.wait_ge(out_ready, n + 1)
                r = n % 2
                rows, up, down = unit(n)
                sp.dma_start(up[1], base[0][r][:, :]).then_inc(out_done[r], 16)
                sp.dma_start(down[1], base[1][r][0:rows, :]).then_inc(out_done[r], 16)
                if n % BATCH == BATCH - 1 and n // U + 1 < MB:
                    load_tables(n // U + 1, n // BATCH % 2)
                if n + 2 < NU:
                    load_base(n + 2)
            for r in range(2):
                sp.wait_ge(out_done[r], 16 * NU)
            for b in range(BATCH):
                row = b * SEQ + SEQ // 2
                sp.dma_start(base[b // 2][b % 2][0:1, :], t["base"][row:row + 1, :]).then_inc(last_in, 16)
            sp.wait_ge(last_ready, 1)
            for b in range(BATCH):
                row = b * SEQ + SEQ // 2
                sp.dma_start(t["out"][row:row + 1, :], base[b // 2][b % 2][0:1, :]).then_inc(last_done, 16)
            sp.wait_ge(last_done, 16 * BATCH)

        @block.tensor
        def _(pe):
            pe.wait_ge(const_in, 16 * 6)
            for m in range(DC + 1):
                dst = (ps_p + ps_q + ps_y[:1])[m]
                if m == DC:
                    pe.wait_ge(brep_ready, 1)
                for k in range(DC):
                    lhs = wout[:, k, m * P:(m + 1) * P] if m < DC else brep[:, k, :]
                    last = pe.matmul(dst[:, :], lhs, dft[:, k, :], start=k == 0, stop=k == DC - 1)
                last.then_inc(w_filled, 1)
            pe.wait_ge(w_emptied, DC + 1)

            def transposes(n, v):
                pe.wait_ge(t_emptied, n * 2 + v + 1)
                hold(pe, sd_ready, n * 2 + v + 3, passed)
                for k in range(DC):
                    last = pe.transpose(ps_t[v][:, k * P:(k + 1) * P], sd[v][:, k * P:(k + 1) * P], ident[:, :])
                last.then_inc(t_filled, 1)

            def project(n, v):
                pe.wait_ge(t_emptied, n * 2 + v + 3)
                pe.wait_ge(y_emptied, n * 2 + v + 1)
                for k in range(DC):
                    last = pe.matmul(ps_y[v][:, :], sdT[v][:, k, :], w2[:, k, :], start=k == 0, stop=k == DC - 1)
                last.then_inc(y_filled, 1)

            transposes(0, 0)
            with pe.Fori(0, NP - 1) as n:
                transposes(n, 1)
                project(n, 0)
                transposes(n + 1, 0)
                project(n, 1)
            transposes(NP - 1, 1)
            project(NP - 1, 0)
            project(NP - 1, 1)
            pe.wait_ge(y_emptied, NP * 2 + 2)

            def turn_rows(n, r):
                pe.wait_ge(turned_ready, n + 1)
                pe.matmul(ps_t[r][:, :], flip[:, :], turned[r][:, :], start=True, stop=True).then_inc(r_filled, 1)

            def chunk(m, first):
                for v in range(2):
                    pe.wait_ge(tab_in[v], m * 32 + 32)
                    for b in range(BATCH):
                        n = m * U + v * BATCH + b
                        for table, dst, c0, c1, free, filled in (
                                (cos[v], ps_p, 0, NCOS, p_emptied, p_filled),
                                (sin[v][:, :, :], ps_q, NCOS, DIM, q_emptied, q_filled)):
                            pe.wait_ge(free, n + 1)
                            for k in range(HT):
                                last = pe.matmul(dst[b % 2][:, 0:c1 - c0], table[:, k, :], y[v][:, b * HT + k, c0:c1],
                                                 start=k == 0, stop=k == HT - 1)
                            last.then_inc(filled, 1)
                        if v or b or not first:
                            turn_rows(n - 1, (b + 1) % 2)

            chunk(0, True)
            with pe.Fori(1, MB) as m:
                chunk(m, False)
            turn_rows(NU - 1, 1)
            pe.wait_ge(p_emptied, NU + 2)
            pe.wait_ge(q_emptied, NU + 2)
            for b in range(BATCH):
                dst = (ps_p + ps_q)[b]
                for k in range(HT):
                    last = pe.matmul(dst[0:1, 0:NCOS], alt[:, :], y[0][:, b * HT + k, 0:NCOS], start=k == 0,
                                     stop=k == HT - 1)
            last.then_inc(last_filled, 1)

        @block.scalar
        def _(act):
            act.sem_inc(q_emptied, 2)
            act.sem_inc(t_emptied, 2)
            for m in range(DC + 1):
                act.wait_ge(w_filled, m + 1)
                src = (ps_p + ps_q + ps_y[:1])[m]
                act.activation(w2[:, m, :] if m < DC else b2[:, :], src[:, :], ACT.Copy, scale=1.0 if m < DC else 2.0)\
                    .then_inc(w_emptied, 1)
            with act.Fori(0, NP) as n:
                for v in range(2):
                    act.wait_ge(t_filled, n * 2 + v + 1)
                    act.wait_ge(y_filled, n * 2 + v + 1)
                    act.copy(sdT[v][:, :, :].rearrange("p k n -> p (k n)"), ps_t[v][:, :]).then_inc(t_emptied, 1)
            act.wait_ge(qs_zeroed, 1)
            with act.Fori(0, NU // 2) as i:
                for r in range(2):
                    act.wait_ge(q_filled, i * 2 + r + 1)
                    act.wait_ge(p_emptied, i * 2 + r + 1)
                    act.copy(qs[r][:, 1:1 + NSIN], ps_q[r][:, 0:NSIN]).then_inc(q_emptied, 1)

        @block.vector
        def _(dve):
            dve.sem_inc(sd_ready, 2)
            dve.sem_inc(y_emptied, 2)
            dve.sem_inc(y_filled, 2)
            dve.sem_inc(p_emptied, 2)
            for r in range(2):
                dve.memset(qs[r][:, :], 0.0)
                last = dve.memset(base[1][r][:, :], 0.0)
            last.then_inc(qs_zeroed, 1)
            dve.wait_ge(const_in, 16 * 6)
            dve.tensor_copy(brep[:, :, :], bcol[:, :, None].broadcast_to([P, DC, P])).then_inc(brep_ready, 1)
            dve.wait_ge(w_emptied, DC + 1)
            def halves(n):
                dve.wait_ge(att_in, n * 32 + 32)
                for v, op in ((0, ALU.add), (1, ALU.subtract)):
                    dve.wait_ge(t_filled, n * 2 + v - 1) if not isinstance(n, int) or n else None
                    dve.tensor_tensor(sd[v][:, :], att[:, 0, :], att[:, 1, :], op).then_inc(sd_ready, 1)

            def project_out(n):
                for v in range(2):
                    dve.wait_ge(y_filled, n * 2 + v + 3)
                    dst = y[v][:, bass.ds(n, 1), :].rearrange("p a c -> p (a c)")
                    if v:
                        dve.tensor_copy(dst, ps_y[v][:, :]).then_inc(y_emptied, 1)
                    else:
                        dve.tensor_tensor(dst, ps_y[v][:, :], b2[:, :], ALU.add).then_inc(y_emptied, 1)

            halves(0)
            with dve.Fori(1, NP) as n:
                halves(n)
                project_out(n - 1)
            project_out(NP - 1)

            def mirror(z):
                return z[:, 1:1 + NSIN][:, ::-1]

            def rows_up(n, r, turn_):
                st = Steps(dve, dve_done, n * 4)
                dve.wait_ge(p_filled, n + 1)
                dve.wait_ge(q_emptied, n + 3)
                st.mark(dve.tensor_tensor(dif[r][:, :], ps_p[r][:, 0:NCOS], qs[r][:, :], ALU.subtract))
                dve.tensor_tensor(turned[r][:, 0:NCOS], ps_p[r][:, 0:NCOS], qs[r][:, :], ALU.add).then_inc(p_emptied, 1)
                st.wait()
                st.mark(dve.tensor_copy(turned[r][:, NCOS:DIM], mirror(dif[r])))
                dve.wait_ge(p_emptied, n + 3)
                st.wait()
                dve.sem_inc(turned_ready, 1)
                dve.wait_ge(base_in[r], turn_ * 32 + 32)
                up = base[0][r]
                st.mark(dve.tensor_tensor(up[:, 0:NCOS], up[:, 0:NCOS], dif[r][:, :], ALU.add))
                st.mark(dve.tensor_tensor(up[:, NCOS:DIM], up[:, NCOS:DIM], mirror(turned[r]), ALU.add))
                st.wait()

            def rows_down(n, r):
                dve.wait_ge(r_filled, n + 1)
                dve.tensor_tensor(base[1][r][:, :], base[1][r][:, :], ps_t[r][:, :], ALU.add).then_inc(out_ready, 1)

            rows_up(0, 0, 0)
            with dve.Fori(0, NU // 2 - 1) as i:
                rows_up(i * 2 + 1, 1, i)
                rows_down(i * 2, 0)
                rows_up(i * 2 + 2, 0, i + 1)
                rows_down(i * 2 + 1, 1)
            rows_up(NU - 1, 1, NU // 2 - 1)
            rows_down(NU - 2, 0)
            rows_down(NU - 1, 1)
            dve.wait_ge(last_filled, 1)
            dve.wait_ge(last_in, 16 * BATCH)
            st = Steps(dve, dve_done, NU * 4)
            for b in range(BATCH):
                row, src = base[b // 2][b % 2], (ps_p + ps_q)[b]
                st.mark(dve.tensor_tensor(row[0:1, 0:NCOS], row[0:1, 0:NCOS], src[0:1, 0:NCOS], ALU.add))
                st.mark(dve.tensor_tensor(row[0:1, NCOS:DIM], row[0:1, NCOS:DIM], src[0:1, 1:1 + NSIN][:, ::-1], ALU.add))
            st.wait()
            dve.sem_inc(last_ready, 1)
def internal(nc):
    def d(name, shape, dt=F32):
        return nc.dram_tensor(f"mid_{name}", shape, dt, kind="Internal").ap()

    return dict(
        xn=d("xn", (TOK, DIM)), q=d("q", (DC, P, TOK)), kc=d("kc", (DC, P, TOK // CF)), vc=d("vc", (TOK // CF, DIM)),
        shared=d("shared", (TOK, DIM)), w=d("w", (P, NTILE * EXPERTS)), pos=d("pos", (P, NTILE * EXPERTS)),
        cnt=d("cnt", (P, EXPERTS)), ids=d("ids", (NSLOT, 1), I32), blk=d("blk", (1, 3 * P), I32),
        slot8=d("slot8", (P, NTILE * TOPK), I32), w8=d("w8", (P, NTILE * TOPK)), rows=d("rows", (NSLOT, DIM)),
        att=d("att", (TOK, DIM)), base=d("base", (TOK, DIM)))


def layout(L0_attn_x, L0_attn_Wqkv, L0_attn_conv_w, L0_attn_conv_b, L0_attn_null_k, L0_attn_null_v, L0_attn_W_out,
           L0_attn_b_out, L0_ffn_router_w, L0_ffn_e_bias, L0_ffn_gate_w, L0_ffn_up_w, L0_ffn_down_w, L0_ffn_sh_gate_w,
           L0_ffn_sh_up_w, L0_ffn_sh_down_w):
    def a(v):
        return np.ascontiguousarray(np.asarray(v, dtype=np.float32))

    def rows(v):
        return np.ascontiguousarray(np.broadcast_to(a(v).reshape(1, -1), (P, a(v).size)))

    conv = a(L0_attn_conv_w).reshape(DC, HPC, DH, DH, CF)
    conv_bd = np.zeros((P, DC, CF, P), np.float32)
    null_k = a(L0_attn_null_k).reshape(DC, HPC, DH)
    null_bd = np.zeros((DC, P, HPC), np.float32)
    for h in range(HPC):
        s = slice(h * DH, (h + 1) * DH)
        conv_bd[s, :, :, s] = conv[:, h].transpose(2, 0, 3, 1)
        null_bd[:, s, h] = null_k[:, h]
    tt = np.arange(SEQ // 2, dtype=np.float64)[:, None]
    k1 = np.arange(SEQ // 2 + 1, dtype=np.float64)[None, :]
    ang = 2 * np.pi * ((tt * k1) % SEQ) / SEQ
    ee = np.arange(DIM, dtype=np.float64)[:, None]
    angd = 2 * np.pi * ((ee * np.arange(DIM // 2 + 1)[None, :]) % DIM) / DIM
    dft_d = np.concatenate([np.cos(angd), np.sin(angd[:, 1:DIM // 2])], axis=1).astype(np.float32)
    def tables(f):
        m = f(ang)[:, :SEQ // 2].reshape(SEQ // 2 // P, P, SEQ // 4 // P, P, 2)
        return np.ascontiguousarray(m.transpose(4, 2, 1, 0, 3)).astype(np.float32)
    return dict(
        x=a(L0_attn_x).reshape(TOK, DIM), wqkv=a(L0_attn_Wqkv), conv_bd=conv_bd,
        conv_b_col=np.ascontiguousarray(a(L0_attn_conv_b).reshape(DC, P).T), conv_b_row=rows(L0_attn_conv_b),
        null_bd=null_bd, null_v_row=rows(L0_attn_null_v), wout_t=np.ascontiguousarray(a(L0_attn_W_out).T),
        b_out_col=np.ascontiguousarray(a(L0_attn_b_out).reshape(DC, P).T),
        router_t=np.ascontiguousarray(a(L0_ffn_router_w).T), e_bias_row=rows(L0_ffn_e_bias),
        gate_w=a(L0_ffn_gate_w), up_w=a(L0_ffn_up_w), down_w=a(L0_ffn_down_w),
        sh_gate=a(L0_ffn_sh_gate_w), sh_up=a(L0_ffn_sh_up_w), sh_down=a(L0_ffn_sh_down_w),
        ident=np.eye(P, dtype=np.float32), tri=np.triu(np.ones((P, P), np.float32), 1), ones=np.ones((P, P), np.float32),
        before=np.ascontiguousarray(np.broadcast_to(np.tril(np.ones((GROUPS, GROUPS), np.float32), -1), (P, GROUPS, GROUPS))),
        bidx=np.arange(3 * P, dtype=np.float32).reshape(P, 3),
        mhalf=np.full((P, TPB), -0.5, np.float32),
        late=np.where(np.arange(P)[:, None] >= CF * np.arange(P // CF)[None, :] + CF - 1, 0.0, -BIG).astype(np.float32),
        cos_t=tables(np.cos), sin_t=tables(np.sin),
        alt=np.ascontiguousarray(np.broadcast_to(np.where(np.arange(P) % 2, -1.0, 1.0)[:, None], (P, 1))).astype(np.float32),
        flip=np.ascontiguousarray(np.eye(P, dtype=np.float32)[::-1]), dft_d=dft_d)


def program(nc, t):
    stage_a(nc, t)
    stage_b(nc, t)
    stage_e(nc, t)
    stage_f(nc, t)
    stage_c(nc, t)


def kernel(**inputs):
    import concourse.bacc as bacc
    from concourse.bass_utils import run_bass_kernel_spmd

    nc = bacc.Bacc("TRN2", target_bir_lowering=False, num_devices=1)
    arrays, aps = {}, internal(nc)
    for name, a in layout(**inputs).items():
        arrays[f"in_{name}"] = a
        aps[name] = nc.dram_tensor(f"in_{name}", a.shape, mybir.dt.from_np(a.dtype), kind="ExternalInput").ap()
    aps["out"] = nc.dram_tensor("out", (TOK, DIM), F32, kind="ExternalOutput").ap()
    program(nc, aps)
    r = run_bass_kernel_spmd(nc, [arrays], core_ids=[0])
    return r.results[0]["out"].reshape(BATCH, SEQ, DIM)
```

```python
from contextlib import ExitStack

import numpy as np

import concourse.bass as bass
from concourse import mybir

F32 = mybir.dt.float32
F32R = mybir.dt.float32r
BF16 = mybir.dt.bfloat16
I32 = mybir.dt.int32
ALU = mybir.AluOpType
ACT = mybir.ActivationFunctionType
AX = mybir.AxisListType.X

P = 128
BATCH, SEQ, DIM = 4, 2048, 512
TOK = BATCH * SEQ
HEADS, DH, CF = 16, 32, 4
NC = SEQ // CF
DC = DIM // P
HPC = P // DH
EXPERTS, TOPK, GROUPS, TOPG = 64, 8, 8, 4
EPG = EXPERTS // GROUPS
HID, HSH = 256, 1024
EPS = 1e-5
SCALE = float(DIM) ** -0.5
BIG = 1e30

TB = 512
TPB = TB // P
NSTEP = TOK // TB
NTILE = TOK // P
CPB = TB // CF

RB = 256
RT = RB // P
SLOTS_USED = TOK * TOPK
NBLK = -(-(SLOTS_USED // RB + EXPERTS - 1) // 2) * 2
NSLOT = NBLK * RB
NCOL = NSLOT // P


def hold(eng, sem, value, passed):
    eng.wait_ge(sem, value)
    eng.sem_inc(passed, 1)


class Steps:

    def __init__(self, eng, sem, base, passed=None):
        self.eng, self.sem, self.base, self.passed, self.n = eng, sem, base, passed, 0

    def mark(self, instruction):
        instruction.then_inc(self.sem, 1)
        self.n += 1
        return instruction

    def wait(self):
        self.eng.wait_ge(self.sem, self.base + self.n)

    def hold(self):
        hold(self.eng, self.sem, self.base + self.n, self.passed)


def opener(nc, ctx, tag=""):
    def sb(name, shape, dt=F32):
        return ctx.enter_context(nc.sbuf_tensor(tag + name, shape, dt))

    def ps(name, shape, dt=F32):
        return ctx.enter_context(nc.psum_tensor(tag + name, shape, dt))

    def sem(name):
        return ctx.enter_context(nc.semaphore(tag + name))

    return sb, ps, sem



A_ORDER = ([("xT", i) for i in range(4)] + [("down", i) for i in range(4)] + [("router", 0)]
           + [("qkv", i) for i in range(12)] + [("kc", 0), ("vc", 0)]
           + [("gu", i) for i in range(16)] + [("pos", 0)])
A_PER = {"xT": 4, "down": 4, "router": 1, "qkv": 12, "kc": 1, "vc": 1, "gu": 16, "pos": 1}


def stage_a(nc, t):
    ctx = ExitStack()
    with ctx:
        sb, ps, sem = opener(nc, ctx)
        wqkv = sb("a_wqkv", [P, DC, 3 * DIM])
        wrt = sb("a_wrt", [P, DC, EXPERTS])
        wconv = sb("a_wconv", [P, DC, CF, P])
        wsg = sb("a_wsg", [P, DC, HSH])
        wsu = sb("a_wsu", [P, DC, HSH])
        wsd = sb("a_wsd", [P, HSH // P, DIM])
        kbias = sb("a_kbias", [P, DC])
        vbias = sb("a_vbias", [P, DIM])
        ebias = sb("a_ebias", [P, EXPERTS])
        ident = sb("a_ident", [P, P])
        trif = sb("a_trif", [P, P])
        tri = sb("a_tri", [P, P], BF16)
        ones = sb("a_ones", [P, P], BF16)
        before = sb("a_before", [P, GROUPS, GROUPS])
        mhalf = sb("a_mhalf", [P, TPB])
        x = sb("a_x", [P, TPB, DIM])
        xn = sb("a_xn", [P, TPB, DIM])
        xT = sb("a_xT", [P, DC, TB])
        qs = sb("a_qs", [P, DC, TB])
        q_hi = sb("a_q_hi", [P, DC, TB], F32R)
        ks = sb("a_ks", [P, DC, CF, CPB])
        vs = sb("a_vs", [P, DC, CF, CPB])
        kcs = sb("a_kcs", [P, DC, CPB])
        kc_hi = sb("a_kc_hi", [P, DC, CPB], F32R)
        vcs = sb("a_vcs", [P, DIM])
        sg = sb("a_sg", [P, 2, TB])
        gated = sb("a_gated", [P, 2, TB])
        hT = sb("a_hT", [P, HSH // P, TB])
        shs = sb("a_shs", [P, TPB, DIM])
        stats = sb("a_stats", [P, TPB, 6])
        mv = sb("a_mv", [P, TPB, 2])
        ve = sb("a_ve", [P, TPB])
        y0 = sb("a_y0", [P, TPB])
        ya = sb("a_ya", [P, TPB])
        yb = sb("a_yb", [P, TPB])
        rstd = sb("a_rstd", [P, TPB])
        NG = TPB * GROUPS
        sc = sb("a_sc", [P, TPB, EXPERTS])
        sbi = sb("a_sbi", [P, TPB, EXPERTS])
        hi4 = sb("a_hi4", [P, NG, 4])
        lo4 = sb("a_lo4", [P, NG, 4])
        hi2 = sb("a_hi2", [P, NG, 2])
        lo2 = sb("a_lo2", [P, NG, 2])
        mi2 = sb("a_mi2", [P, NG, 2])
        hi1 = sb("a_hi1", [P, NG])
        lo1 = sb("a_lo1", [P, NG])
        mi1 = sb("a_mi1", [P, NG])
        grp = sb("a_grp", [P, NG])
        cgt = sb("a_cgt", [P, TPB, GROUPS, GROUPS])
        ceq = sb("a_ceq", [P, TPB, GROUPS, GROUPS])
        rank = sb("a_rank", [P, NG])
        gkeep = sb("a_gkeep", [P, NG])
        masked = sb("a_masked", [P, TPB, EXPERTS])
        best = sb("a_best", [P, TPB, 8])
        taken = sb("a_taken", [P, TPB, EXPERTS])
        sel = sb("a_sel", [P, TPB, EXPERTS])
        selb = sb("a_selb", [P, TPB, EXPERTS], BF16)
        wsum = sb("a_wsum", [P, TPB])
        winv = sb("a_winv", [P, TPB])
        w = sb("a_w", [P, TPB, EXPERTS])
        posm = sb("a_posm", [P, TPB, EXPERTS])
        ptmp = sb("a_ptmp", [P, TPB, EXPERTS])
        carry = sb("a_carry", [P, EXPERTS])
        bank = [ps(f"a_bank{i}", [P, 512]) for i in range(8)]

        w_in = sem("a_w_in")
        late_w_in = sem("a_late_w_in")
        x_in = sem("a_x_in")
        passed = t["passed"]
        q_split = sem("a_q_split")
        kc_split = sem("a_kc_split")
        const_ready = sem("a_const_ready")
        dve_done = sem("a_dve_done")
        var_ready = sem("a_var_ready")
        pow_ready = sem("a_pow_ready")
        xn_ready = sem("a_xn_ready")
        route_ready = sem("a_route_ready")
        scores_ready = sem("a_scores_ready")
        sig_ready = sem("a_sig_ready")
        hT_ready = sem("a_hT_ready")
        xn_out = sem("a_xn_out")
        q_out = sem("a_q_out")
        kc_out = sem("a_kc_out")
        vc_out = sem("a_vc_out")
        wp_out = sem("a_wp_out")
        sh_out = sem("a_sh_out")
        filled = {k: sem(f"a_filled_{k}") for k in A_PER}
        emptied = {k: sem(f"a_emptied_{k}") for k in A_PER}

        def nth(kind, step, i):
            done_before = (step - 1 if kind == "down" else step) * A_PER[kind]
            return done_before + i + 1

        NLOADS = 10
        block = ctx.enter_context(nc.Block())

        @block.sync
        def _(sp):
            def load_x(s):
                sp.dma_start(x[:, :, :], t["x"][bass.ds(s * TB, TB), :].rearrange("(i p) c -> p i c", p=P))\
                    .then_inc(x_in, 16)

            def load_weights(pairs, signal):
                for dst, src in pairs:
                    sp.dma_start(dst[:, :, :], src.rearrange("(k p) n -> p k n", p=P)).then_inc(signal, 16)

            load_x(0)
            for dst, src in ((ident, t["ident"]), (trif, t["tri"]), (mhalf, t["mhalf"]), (kbias, t["conv_b_col"]),
                             (vbias, t["conv_b_row"]), (ebias, t["e_bias_row"])):
                sp.dma_start(dst[:, :], src).then_inc(w_in, 16)
            sp.dma_start(before[:, :, :], t["before"]).then_inc(w_in, 16)
            sp.dma_start(sel[:, :, :].rearrange("p a e -> p (a e)")[:, 0:P], t["ones"]).then_inc(w_in, 16)
            load_weights(((wrt, t["router_t"]), (wqkv, t["wqkv"])), w_in)
            sp.dma_start(wconv[:, :, :, :], t["conv_bd"]).then_inc(late_w_in, 16)
            load_weights(((wsg, t["sh_gate"]), (wsu, t["sh_up"]), (wsd, t["sh_down"])), late_w_in)

            def step(s, first, last):
                if not last:
                    hold(sp, xn_ready, (s + 1) * TPB, passed)
                    load_x(s + 1)
                else:
                    hold(sp, xn_ready, (s + 1) * TPB, passed)
                sp.dma_start(t["xn"][bass.ds(s * TB, TB), :].rearrange("(i p) c -> p i c", p=P), xn[:, :, :])\
                    .then_inc(xn_out, 16)
                if not first:
                    store_shared(s - 1)
                hold(sp, q_split, s * 2 + 2, passed)
                for dst, src in ((t["q_lo"], qs[:, :, :]), (t["q_hi"], q_hi[:, :, :].bitcast(F32))):
                    sp.dma_start(dst[:, :, bass.ds(s * TB, TB)].rearrange("c p n -> p c n"), src).then_inc(q_out, 16)
                hold(sp, kc_split, s * 2 + 2, passed)
                for dst, src in ((t["kc_lo"], kcs[:, :, :]), (t["kc_hi"], kc_hi[:, :, :].bitcast(F32))):
                    sp.dma_start(dst[:, :, bass.ds(s * CPB, CPB)].rearrange("c p n -> p c n"), src).then_inc(kc_out, 16)
                hold(sp, emptied["vc"], nth("vc", s, 0), passed)
                sp.dma_start(t["vc"][bass.ds(s * CPB, CPB), :], vcs[:, :]).then_inc(vc_out, 16)
                hold(sp, emptied["pos"], nth("pos", s, 0), passed)
                sp.dma_start(t["pos"][:, bass.ds(s * TPB * EXPERTS, TPB * EXPERTS)],
                             posm[:, :, :].rearrange("p a e -> p (a e)")).then_inc(wp_out, 16)
                sp.dma_start(t["w"][:, bass.ds(s * TPB * EXPERTS, TPB * EXPERTS)],
                             w[:, :, :].rearrange("p a e -> p (a e)")).then_inc(wp_out, 16)

            def store_shared(s):
                hold(sp, emptied["down"], (s + 1) * 4, passed)
                sp.dma_start(t["shared"][bass.ds(s * TB, TB), :].rearrange("(i p) c -> p i c", p=P), shs[:, :, :])\
                    .then_inc(sh_out, 16)

            step(0, True, False)
            with sp.Fori(1, NSTEP - 1) as s:
                step(s, False, False)
            step(NSTEP - 1, False, True)
            store_shared(NSTEP - 1)
            sp.dma_start(t["cnt"], carry[:, :]).then_inc(sh_out, 16)
            for s_, n in ((xn_out, 1), (q_out, 2), (kc_out, 2), (vc_out, 1), (wp_out, 2)):
                sp.wait_ge(s_, 16 * n * NSTEP)
            sp.wait_ge(sh_out, 16 * (NSTEP + 1))

        @block.gpsimd
        def _(pool):
            pool.wait_ge(w_in, 16 * NLOADS)

            def inv_sqrt(s):
                pool.wait_ge(var_ready, s + 1)
                pool.tensor_tensor(y0[:, :], ve[:, :], mhalf[:, :], ALU.pow).then_inc(pow_ready, 1)

            def split(ready, count, x, hi, done, s):
                hold(pool, ready, count, passed)
                pool.tensor_copy(hi[:, :, :], x[:, :, :]).then_inc(done, 1)
                pool.wait_ge(done, s * 2 + 1)
                pool.tensor_tensor(x[:, :, :], x[:, :, :], hi[:, :, :].bitcast(F32), ALU.subtract).then_inc(done, 1)

            def splits(s):
                split(emptied["qkv"], nth("qkv", s, 3), qs, q_hi, q_split, s)
                split(emptied["kc"], nth("kc", s, 0), kcs, kc_hi, kc_split, s)

            inv_sqrt(0)
            with pool.Fori(0, NSTEP - 1) as s:
                inv_sqrt(s + 1)
                splits(s)
            splits(NSTEP - 1)

        @block.scalar
        def _(act):
            def step(s, first, last):
                for k in range(DC):
                    act.wait_ge(filled["xT"], nth("xT", s, k))
                    act.copy(xT[:, k, :], bank[k][:, :]).then_inc(emptied["xT"], 1)
                act.wait_ge(filled["router"], nth("router", s, 0))
                if not first:
                    act.wait_ge(route_ready, s)
                act.activation(sc[:, :, :].rearrange("p a e -> p (a e)"), bank[A_BANK[("router", 0)]][:, 0:TPB * EXPERTS],
                               ACT.Sigmoid).then_inc(emptied["router"], 1)
                for i in range(12):
                    act.wait_ge(filled["qkv"], nth("qkv", s, i))
                    src = bank[A_BANK[("qkv", i)]]
                    if i == 0 and not first:
                        act.wait_ge(q_out, 32 * s)
                    if i < 4:
                        act.copy(qs[:, i, :], src[:, :]).then_inc(emptied["qkv"], 1)
                    else:
                        dst = ks if i < 8 else vs
                        act.copy(dst[:, i % 4, :, :], src[:, :].rearrange("p (j c) -> p c j", c=CF))\
                            .then_inc(emptied["qkv"], 1)
                act.wait_ge(filled["kc"], nth("kc", s, 0))
                if not first:
                    act.wait_ge(kc_out, 32 * s)
                for k in range(DC):
                    last_i = act.activation(kcs[:, k, :], bank[A_BANK[("kc", 0)]][:, k * CPB:(k + 1) * CPB], ACT.Identity,
                                            bias=kbias[:, k:k + 1])
                last_i.then_inc(emptied["kc"], 1)
                for j in range(8):
                    act.wait_ge(filled["gu"], nth("gu", s, 2 * j))
                    if j >= 2 or not first:
                        act.wait_ge(emptied["gu"], nth("gu", s, 2 * j - 3))
                    act.activation(sg[:, j % 2, :], bank[A_BANK[("gu", 2 * j)]][:, :], ACT.Sigmoid)\
                        .then_inc(sig_ready, 1)

            act.wait_ge(w_in, 16 * NLOADS)
            step(0, True, False)
            with act.Fori(1, NSTEP) as s:
                step(s, False, False)

        @block.vector
        def _(dve):
            def layernorm(s, st, first):
                dve.wait_ge(x_in, 16 * (s + 1))
                for i in range(TPB):
                    st.mark(dve.bn_stats(stats[:, i, :], x[:, i, :]))
                st.hold()
                for i in range(TPB):
                    st.mark(dve.bn_aggr(mv[:, i, :], stats[:, i, :]))
                st.wait()
                dve.tensor_scalar(ve[:, :], mv[:, :, 1], EPS, None, ALU.add).then_inc(var_ready, 1)
                dve.wait_ge(pow_ready, s + 1)
                st.mark(dve.tensor_tensor(ya[:, :], y0[:, :], y0[:, :], ALU.mult))
                st.wait()
                st.mark(dve.tensor_tensor(yb[:, :], ya[:, :], ve[:, :], ALU.mult))
                st.wait()
                st.mark(dve.tensor_scalar(ya[:, :], yb[:, :], -0.5, 1.5, ALU.mult, ALU.add))
                st.wait()
                st.mark(dve.tensor_tensor(rstd[:, :], ya[:, :], y0[:, :], ALU.mult))
                st.wait()
                if not first:
                    dve.wait_ge(filled["xT"], 4 * s)
                    dve.wait_ge(xn_out, 16 * s)
                for i in range(TPB):
                    dve.tensor_scalar(xn[:, i, :], x[:, i, :], mv[:, i, 0:1], rstd[:, i:i + 1], ALU.subtract, ALU.mult)\
                        .then_inc(xn_ready, 1)

            def route(s, st, first):
                def tt(out, a, b, op):
                    return st.mark(dve.tensor_tensor(out, a, b, op))

                dve.wait_ge(emptied["router"], nth("router", s, 0))
                tt(sbi[:, :, :], sc[:, :, :], ebias[:, None, :].broadcast_to([P, TPB, EXPERTS]), ALU.add)
                st.wait()
                v = sbi[:, :, :].rearrange("p a (g e) -> p (a g) e", e=EPG)
                tt(hi4[:, :, :], v[:, :, 0:4], v[:, :, 4:8], ALU.max)
                tt(lo4[:, :, :], v[:, :, 0:4], v[:, :, 4:8], ALU.min)
                st.wait()
                tt(hi2[:, :, :], hi4[:, :, 0:2], hi4[:, :, 2:4], ALU.max)
                tt(mi2[:, :, :], hi4[:, :, 0:2], hi4[:, :, 2:4], ALU.min)
                tt(lo2[:, :, :], lo4[:, :, 0:2], lo4[:, :, 2:4], ALU.max)
                st.wait()
                tt(lo2[:, :, :], lo2[:, :, :], mi2[:, :, :], ALU.max)
                tt(hi1[:, :], hi2[:, :, 0], hi2[:, :, 1], ALU.max)
                tt(mi1[:, :], hi2[:, :, 0], hi2[:, :, 1], ALU.min)
                st.wait()
                tt(lo1[:, :], lo2[:, :, 0], lo2[:, :, 1], ALU.max)
                st.wait()
                tt(lo1[:, :], lo1[:, :], mi1[:, :], ALU.max)
                st.wait()
                tt(grp[:, :], hi1[:, :], lo1[:, :], ALU.add)
                st.wait()
                shape = [P, TPB, GROUPS, GROUPS]
                g3 = grp[:, :].rearrange("p (a g) -> p a g", g=GROUPS)
                other = g3[:, :, None, :].broadcast_to(shape)
                own = g3[:, :, :, None].broadcast_to(shape)
                tt(cgt[:, :, :, :], other, own, ALU.is_gt)
                tt(ceq[:, :, :, :], other, own, ALU.is_equal)
                st.wait()
                tt(ceq[:, :, :, :], ceq[:, :, :, :], before[:, None, :, :].broadcast_to(shape), ALU.mult)
                st.wait()
                tt(cgt[:, :, :, :], cgt[:, :, :, :], ceq[:, :, :, :], ALU.add)
                st.wait()
                st.mark(dve.tensor_reduce(rank[:, :], cgt[:, :, :, :].rearrange("p a g o -> p (a g) o"), AX, ALU.add))
                st.wait()
                st.mark(dve.tensor_scalar(gkeep[:, :], rank[:, :], float(TOPG), -1.0, ALU.is_lt, ALU.add))
                st.wait()
                st.mark(dve.scalar_tensor_tensor(
                    masked[:, :, :].rearrange("p a (g e) -> p (a g) e", e=EPG),
                    gkeep[:, :, None].broadcast_to([P, NG, EPG]), BIG, v, ALU.mult, ALU.add))
                st.hold()
                for i in range(TPB):
                    st.mark(dve.max(best[:, i, :], masked[:, i, :]))
                st.hold()
                for i in range(TPB):
                    st.mark(dve.match_replace(taken[:, i, :], best[:, i, :], masked[:, i, :], -3e38))
                st.wait()
                if not first:
                    dve.wait_ge(wp_out, 32 * s)
                tt(sel[:, :, :], taken[:, :, :], masked[:, :, :], ALU.not_equal)
                st.wait()
                st.mark(dve.tensor_copy(selb[:, :, :], sel[:, :, :]))
                tt(w[:, :, :], sc[:, :, :], sel[:, :, :], ALU.mult)
                st.wait()
                st.mark(dve.tensor_reduce(wsum[:, :], w[:, :, :], AX, ALU.add))
                st.wait()
                st.mark(dve.tensor_scalar(wsum[:, :], wsum[:, :], 1e-20, None, ALU.add))
                st.wait()
                st.mark(dve.reciprocal(winv[:, :], wsum[:, :]))
                st.wait()
                dve.tensor_tensor(w[:, :, :], w[:, :, :], winv[:, :, None].broadcast_to([P, TPB, EXPERTS]), ALU.mult)\
                    .then_inc(route_ready, 1)

            def down_out(s, first):
                for i in range(4):
                    dve.wait_ge(filled["down"], 4 * s + i + 1)
                    if i == 0 and not first:
                        dve.wait_ge(sh_out, 16 * s)
                    dve.tensor_copy(shs[:, i, :], bank[A_BANK[("down", i)]][:, :]).then_inc(emptied["down"], 1)

            def step(s, first, last, second=False):
                st = Steps(dve, dve_done, s * STEP_MARKS + LN_MARKS + 3, passed)
                if not first:
                    down_out(s - 1, second)
                if not last:
                    layernorm(s + 1, st, False)
                route(s, st, first)
                dve.wait_ge(filled["vc"], nth("vc", s, 0))
                if not first:
                    dve.wait_ge(vc_out, 16 * s)
                dve.tensor_tensor(vcs[:, :], bank[A_BANK[("vc", 0)]][:, :], vbias[:, :], ALU.add)\
                    .then_inc(emptied["vc"], 1)
                for j in range(8):
                    dve.wait_ge(sig_ready, s * 8 + j + 1)
                    dve.tensor_tensor(gated[:, j % 2, :], sg[:, j % 2, :], bank[A_BANK[("gu", 2 * j)]][:, :], ALU.mult)\
                        .then_inc(emptied["gu"], 1)
                    dve.wait_ge(filled["gu"], nth("gu", s, 2 * j + 1))
                    dve.wait_ge(emptied["gu"], nth("gu", s, 2 * j))
                    if j == 0 and not first:
                        dve.wait_ge(filled["down"], nth("down", s, 3))
                    dve.tensor_tensor(hT[:, j, :], gated[:, j % 2, :], bank[A_BANK[("gu", 2 * j + 1)]][:, :], ALU.mult)\
                        .then_inc(emptied["gu"], 1)
                dve.wait_ge(filled["pos"], nth("pos", s, 0))
                pb = bank[A_BANK[("pos", 0)]]
                st.mark(dve.scalar_tensor_tensor(
                    ptmp[:, :, :], pb[:, 0:TPB * EXPERTS].rearrange("p (a e) -> p a e", a=TPB), 1.0,
                    carry[:, None, :].broadcast_to([P, TPB, EXPERTS]), ALU.add, ALU.add))
                st.wait()
                st.mark(dve.tensor_tensor(posm[:, :, :], ptmp[:, :, :], sel[:, :, :], ALU.mult))
                st.mark(dve.tensor_tensor(carry[:, :], carry[:, :], pb[:, TPB * EXPERTS:(TPB + 1) * EXPERTS], ALU.add))
                st.wait()
                dve.sem_inc(emptied["pos"], 1)
                if last:
                    assert st.n == STEP_MARKS - LN_MARKS, st.n
                else:
                    assert st.n == STEP_MARKS, st.n

            LN_MARKS = 2 * TPB + 4
            STEP_MARKS = LN_MARKS + 28 + 2 * TPB
            dve.wait_ge(w_in, 16 * NLOADS)
            s0 = Steps(dve, dve_done, 0, passed)
            s0.mark(dve.memset(carry[:, :], 0.0))
            s0.mark(dve.tensor_copy(ones[:, :], sel[:, :, :].rearrange("p a e -> p (a e)")[:, 0:P]))
            s0.mark(dve.tensor_copy(tri[:, :], trif[:, :]))
            s0.wait()
            dve.sem_inc(const_ready, 1)
            layernorm(0, s0, True)
            step(0, True, False)
            step(1, False, False, second=True)
            with dve.Fori(2, NSTEP - 1) as s:
                step(s, False, False)
            step(NSTEP - 1, False, True)
            down_out(NSTEP - 1, False)

        @block.tensor
        def _(pe):
            def bank_free(kind, i, s, first):
                g = A_ORDER.index((kind, i))
                if g >= 8:
                    k, o = A_ORDER[g - 8]
                    if not (first and k == "down"):
                        pe.wait_ge(emptied[k], nth(k, s, o))
                elif not first:
                    k, o = A_ORDER[g + len(A_ORDER) - 8]
                    pe.wait_ge(emptied[k], nth(k, s - 1, o))
                return bank[A_BANK[(kind, i)]]

            def down(s, first, bank_wait):
                pe.wait_ge(emptied["gu"], 16 * (s + 1))
                for i in range(TPB):
                    b = bank_wait(i)
                    for j in range(HSH // P):
                        last_i = pe.matmul(b[:, :], hT[:, j, i * P:(i + 1) * P], wsd[:, j, :], start=j == 0,
                                           stop=j == HSH // P - 1)
                    last_i.then_inc(filled["down"], 1)

            def step(s, first):
                for k in range(DC):
                    b = bank_free("xT", k, s, first)
                    if k == 0:
                        pe.wait_ge(xn_ready, TPB * (s + 1))
                    for i in range(TPB):
                        last_i = pe.transpose(b[:, i * P:(i + 1) * P], xn[:, i, k * P:(k + 1) * P], ident[:, :])
                    last_i.then_inc(filled["xT"], 1)
                if not first:
                    down(s - 1, False, lambda i: bank_free("down", i, s, False))
                b = bank_free("router", 0, s, first)
                pe.wait_ge(emptied["xT"], nth("xT", s, DC - 1))
                for i in range(TPB):
                    for k in range(DC):
                        last_i = pe.matmul(b[:, i * EXPERTS:(i + 1) * EXPERTS], xT[:, k, i * P:(i + 1) * P], wrt[:, k, :],
                                           start=k == 0, stop=k == DC - 1)
                last_i.then_inc(filled["router"], 1)
                for m in range(12):
                    b = bank_free("qkv", m, s, first)
                    for k in range(DC):
                        last_i = pe.matmul(b[:, :], wqkv[:, k, m * P:(m + 1) * P], xT[:, k, :], start=k == 0,
                                           stop=k == DC - 1)
                    last_i.then_inc(filled["qkv"], 1)
                b = bank_free("kc", 0, s, first)
                pe.wait_ge(emptied["qkv"], nth("qkv", s, 11))
                if first:
                    pe.wait_ge(late_w_in, 16 * 4)
                for k in range(DC):
                    for c in range(CF):
                        last_i = pe.matmul(b[:, k * CPB:(k + 1) * CPB], wconv[:, k, c, :], ks[:, k, c, :], start=c == 0,
                                           stop=c == CF - 1)
                last_i.then_inc(filled["kc"], 1)
                b = bank_free("vc", 0, s, first)
                for k in range(DC):
                    for c in range(CF):
                        last_i = pe.matmul(b[:, k * P:(k + 1) * P], vs[:, k, c, :], wconv[:, k, c, :], start=c == 0,
                                           stop=c == CF - 1)
                last_i.then_inc(filled["vc"], 1)
                for j in range(HSH // P):
                    for i, wt in ((2 * j, wsg), (2 * j + 1, wsu)):
                        b = bank_free("gu", i, s, first)
                        for k in range(DC):
                            last_i = pe.matmul(b[:, :], wt[:, k, j * P:(j + 1) * P], xT[:, k, :], start=k == 0,
                                               stop=k == DC - 1)
                        last_i.then_inc(filled["gu"], 1)
                b = bank_free("pos", 0, s, first)
                pe.wait_ge(route_ready, s + 1)
                for i in range(TPB + 1):
                    dst = b[:, i * EXPERTS:(i + 1) * EXPERTS]
                    for n in range(min(i + 1, TPB)):
                        last_i = pe.matmul(dst, (tri if n == i else ones)[:, :], selb[:, n, :], start=n == 0,
                                           stop=n == min(i + 1, TPB) - 1)
                last_i.then_inc(filled["pos"], 1)

            pe.wait_ge(w_in, 16 * NLOADS)
            pe.wait_ge(const_ready, 1)
            step(0, True)
            with pe.Fori(1, NSTEP) as s:
                step(s, False)
            down(NSTEP - 1, False, lambda i: bank_free("down", i, NSTEP, False))


A_BANK = {g: i % 8 for i, g in enumerate(A_ORDER)}




KW = P // CF
QT = SEQ // P
PAIRS = HPC // 2
UNITS = QT * PAIRS


class Attention:

    def __init__(self, nc, ctx, t, b0, nb, tag, passed):
        self.t, self.b0, self.nb, self.items = t, b0, nb, nb * DC
        sb, ps, sem = opener(nc, ctx, tag)
        self.q = [sb(f"q{s}", [3 * DH, HPC, SEQ], F32R) for s in range(2)]
        self.kc = [sb(f"kc{s}", [3 * DH, HPC, 2 + NC], F32R) for s in range(2)]
        self.null_raw = sb("null_raw", [3 * DH, (DC + 1) * HPC * 2])
        self.null = sb("null", [3 * DH, (DC + 1) * HPC * 2], F32R)
        self.vc = [sb(f"vc{s}", [P, NC // P, P]) for s in range(2)]
        self.nullv = sb("nullv", [P, DIM])
        self.late = sb("late", [P, KW])
        self.ident = sb("ident", [P, P])
        self.p = [sb(f"p{r}", [P, 2, NC]) for r in range(2)]
        self.pT = [sb(f"pT{r}", [P, 2, NC]) for r in range(2)]
        self.mx = sb("mx", [P, 2, 2])
        self.oT = [sb(f"oT{r}", [P, P]) for r in range(2)]
        self.s0n = [sb(f"s0n{s}", [P, QT, HPC]) for s in range(2)]
        self.nm = [sb(f"nm{s}", [P, QT, HPC]) for s in range(2)]
        self.rs = [sb(f"rs{s}", [P, QT, HPC]) for s in range(2)]
        self.d0 = sb("d0", [P, QT, HPC])
        self.p0 = sb("pnull", [P, QT, HPC])
        self.den = sb("den", [P, QT, HPC])
        self.rden = sb("rden", [P, QT, HPC])
        self.raw = [sb(f"raw{s}", [P, QT, P]) for s in range(2)]
        self.nulls = sb("nulls", [P, QT, P])
        self.ps_s = [ps(f"ps_s{r}", [P, 2, 512]) for r in range(2)]
        self.ps_t = [ps(f"ps_t{h}", [P, 512]) for h in range(2)]
        self.ps_o = [ps(f"ps_o{r}", [P, 512]) for r in range(2)]
        self.const_in = sem("const_in")
        self.item_in = [sem(f"item_in{s}") for s in range(2)]
        self.zeroed = sem("zeroed")
        self.passed = passed
        self.null_ready = sem("null_ready")
        self.s_filled = sem("s_filled")
        self.s_emptied = sem("s_emptied")
        self.nm_ready = sem("nm_ready")
        self.p_transposed = sem("p_transposed")
        self.t0_emptied = sem("t0_emptied")
        self.t1_emptied = sem("t1_emptied")
        self.pv_done = sem("pv_done")
        self.oT_ready = sem("oT_ready")
        self.o_turned = sem("o_turned")
        self.o_emptied = sem("o_emptied")
        self.dve_done = sem("dve_done")
        self.d0_ready = sem("d0_ready")
        self.p0_ready = sem("p0_ready")
        self.raw_ready = sem("raw_ready")
        self.att_out = [sem(f"att_out{s}") for s in range(2)]

    def each_item(self, eng):
        with eng.Fori(0, self.nb) as b:
            with eng.Fori(0, DC // 2) as c2:
                for s in range(2):
                    yield s, b * DC + c2 * 2 + s, b, c2

    def sync(self, sp, side=None):
        t = self.t
        for dst, src in ((self.nullv, t["null_v_row"]), (self.late, t["late"]), (self.ident, t["ident"])):
            sp.dma_start(dst[:, :], src).then_inc(self.const_in, 16)
        sp.dma_start(self.null_raw[:, :], t["null_rows"]).then_inc(self.const_in, 16)

        def load(g):
            s, b, c = g % 2, self.b0 + g // DC, g % DC
            if g >= 2:
                sp.wait_ge(self.pv_done, (g - 1) * UNITS + 2)
            for dst, n, parts in ((self.q, SEQ, ("q_hi", "q_hi", "q_lo")), (self.kc, NC, ("kc_hi", "kc_lo", "kc_hi"))):
                skip = 2 if dst is self.kc else 0
                for i, part in enumerate(parts):
                    sp.dma_start(dst[s][i * DH:(i + 1) * DH, :, skip:].bitcast(F32),
                                 t[part][c, :, b * n:(b + 1) * n].rearrange("(h r) n -> r h n", r=DH))\
                        .then_inc(self.item_in[s], 16)
            sp.dma_start(self.vc[s][:, :, :],
                         t["vc"][b * NC:(b + 1) * NC, c * P:(c + 1) * P].rearrange("(n p) d -> p n d", p=P))\
                .then_inc(self.item_in[s], 16)

        load(0)
        sp.wait_ge(self.item_in[0], 16 * 7)
        load(1)
        for g in range(self.items):
            if side:
                side(g)
            if g + 2 < self.items:
                load(g + 2)
            sp.wait_ge(self.raw_ready, g + 1)
            b, c = self.b0 + g // DC, g % DC
            sp.dma_start(t["att"][b * SEQ:(b + 1) * SEQ, c * P:(c + 1) * P].rearrange("(i p) d -> p i d", p=P),
                         self.raw[g % 2][:, :, :]).then_inc(self.att_out[g % 2], 16)
        for s in range(2):
            sp.wait_ge(self.att_out[s], 16 * (self.items // 2 + 1))

    def scores(self, m, w):
        return self.ps_s[m % 2][:, :, 2:2 + w] if w < NC else self.ps_s[m % 2][:, :, :]

    def tensor(self, pe):
        pe.wait_ge(self.const_in, 16 * 4)
        pe.wait_ge(self.zeroed, 3)
        pe.sem_inc(self.p_transposed, 2)
        pe.sem_inc(self.pv_done, 2)
        for s, g, b, c2 in self.each_item(pe):
            pe.wait_ge(self.item_in[s], (b * (DC // 2) + c2 + 1) * 16 * 7)
            pe.wait_ge(self.null_ready, g + 1)
            for m in range(UNITS + 3):
                if m < UNITS:
                    i, w = m // PAIRS, KW * (m // PAIRS + 1)
                    pe.wait_ge(self.s_emptied, g * UNITS + m + 1)
                    for h in range(2):
                        head = m % PAIRS * 2 + h
                        q = self.q[s][:, head, i * P:(i + 1) * P]
                        if w == NC - KW:
                            pe.matmul(self.ps_s[m % 2][:, h, NC - 2:NC], self.q[s][:, head, (i + 1) * P:(i + 2) * P],
                                      self.kc[s][:, head, 0:2], start=True, stop=True)
                        if w < NC:
                            last = pe.matmul(self.ps_s[m % 2][:, h, 0:w + 2], q, self.kc[s][:, head, 0:w + 2],
                                             start=True, stop=True)
                        else:
                            last = pe.matmul(self.ps_s[m % 2][:, h, 0:w], q, self.kc[s][:, head, 2:2 + w],
                                             start=True, stop=True)
                    last.then_inc(self.s_filled, 1)
                if 1 <= m <= UNITS:
                    u = m - 1
                    w = KW * (u // PAIRS + 1)
                    pe.wait_ge(self.s_emptied, g * UNITS + u + 3)
                    pe.wait_ge(self.t0_emptied, g * UNITS + u + 1)
                    hold(pe, self.t1_emptied, g * UNITS + u + 1, self.passed)
                    for h in range(2):
                        for k0 in range(0, w, P):
                            kw = min(P, w - k0)
                            last = pe.transpose(self.ps_t[h][0:kw, k0:k0 + P], self.p[u % 2][:, h, k0:k0 + kw],
                                                self.ident[:, :])
                    last.then_inc(self.p_transposed, 1)
                if m >= 4 and m % PAIRS == 0:
                    i = (m - 4) // PAIRS
                    o = self.ps_o[(s + i + 1) % 2]
                    pe.wait_ge(self.oT_ready, g * QT + i + 1)
                    pe.transpose(o[:, P:2 * P], self.oT[i % 2][:, :], self.ident[:, :]).then_inc(self.o_turned, 1)
                if 2 <= m < UNITS + 2:
                    u = m - 2
                    i, w = u // PAIRS, KW * (u // PAIRS + 1)
                    pe.wait_ge(self.t0_emptied, g * UNITS + u + 2)
                    pe.wait_ge(self.t1_emptied, g * UNITS + u + 2)
                    o = self.ps_o[(s + i + 1) % 2]
                    if u % PAIRS == 0:
                        pe.wait_ge(self.o_emptied, g * QT + (2 if i == 0 else i + 1))
                    if w < P:
                        pe.sem_inc(self.passed, 1)
                    for h in range(2):
                        head = slice((u % PAIRS * 2 + h) * DH, (u % PAIRS * 2 + h + 1) * DH)
                        for k0 in range(0, w, P):
                            kw = min(P, w - k0)
                            last = pe.matmul(o[head, 0:P], self.vc[s][0:kw, k0 // P, head],
                                             self.pT[u % 2][0:kw, h, k0:k0 + P], start=k0 == 0, stop=k0 + P >= w)
                    last.then_inc(self.pv_done, 1)

    def pT_out(self, eng, copy, h, g, u, emptied):
        w = KW * (u // PAIRS + 1)
        n = -(-w // P) * P
        eng.wait_ge(self.p_transposed, g * UNITS + u + 3)
        eng.wait_ge(self.pv_done, g * UNITS + u + 1)
        copy(self.pT[u % 2][:, h, 0:n], self.ps_t[h][:, 0:n]).then_inc(emptied, 1)

    def scalar(self, act):
        act.sem_inc(self.s_emptied, 2)
        act.sem_inc(self.t1_emptied, 1)
        act.sem_inc(self.o_emptied, 2)
        for s, g, b, c2 in self.each_item(act):
            for m in range(UNITS + 3):
                if 1 <= m <= UNITS:
                    self.pT_out(act, act.copy, 1, g, m - 1, self.t1_emptied)
                if m < UNITS:
                    i, w, h0 = m // PAIRS, KW * (m // PAIRS + 1), m % PAIRS * 2
                    act.wait_ge(self.nm_ready, g * UNITS + m + 1)
                    act.wait_ge(self.p_transposed, g * UNITS + m + 1)
                    for h in range(2):
                        last = act.activation(self.p[m % 2][:, h, 0:w], self.scores(m, w)[:, h, :], ACT.Exp,
                                              bias=self.nm[s][:, i, h0 + h:h0 + h + 1], scale=SCALE,
                                              accum_out=self.rs[s][:, i, h0 + h:h0 + h + 1])
                    last.then_inc(self.s_emptied, 1)
                if m >= 4 and m % PAIRS == 0:
                    i = (m - 4) // PAIRS
                    if i == 0:
                        act.wait_ge(self.att_out[s], (b * (DC // 2) + c2 + 1) * 16)
                    act.wait_ge(self.o_turned, g * QT + i + 1)
                    act.copy(self.raw[s][:, i, :], self.ps_o[(s + i + 1) % 2][:, P:2 * P]).then_inc(self.o_emptied, 1)
                if m >= 3 and m % PAIRS == 1:
                    i = (m - 3) // PAIRS
                    act.wait_ge(self.pv_done, g * UNITS + 2 * i + 4)
                    act.copy(self.oT[i % 2][:, :], self.ps_o[(s + i + 1) % 2][:, 0:P]).then_inc(self.oT_ready, 1)
            act.wait_ge(self.d0_ready, g + 1)
            act.activation(self.p0[:, :, :], self.d0[:, :, :], ACT.Exp).then_inc(self.p0_ready, 1)

    MARKS = 3 * UNITS + 4

    def vector(self, dve, side):
        for h in range(2):
            last = dve.memset(self.ps_t[h][:, :], 0.0)
        last.then_inc(self.zeroed, 1)
        dve.wait_ge(self.const_in, 16 * 4)
        dve.tensor_copy(self.null[:, :], self.null_raw[:, :]).then_inc(self.zeroed, 1)
        dve.wait_ge(self.zeroed, 2)
        lo = slice(DH, 2 * DH)
        dve.tensor_tensor(self.null[lo, :], self.null_raw[lo, :], self.null[lo, :].bitcast(F32), ALU.subtract)\
            .then_inc(self.zeroed, 1)
        dve.wait_ge(self.zeroed, 3)

        def place_null(c, s):
            n = HPC * 2
            dve.tensor_copy(self.kc[s][:, :, 0:2], self.null[:, bass.ds(c * n, n)].bitcast(F32)
                            .rearrange("p (h a) -> p h a", a=2)).then_inc(self.null_ready, 1)

        place_null(0, 0)
        dve.sem_inc(self.t0_emptied, 1)
        dve.sem_inc(self.att_out[0], 16)
        dve.sem_inc(self.att_out[1], 16)
        for s, g, b, c2 in self.each_item(dve):
            st = Steps(dve, self.dve_done, g * self.MARKS)
            for m in range(UNITS + 1):
                if m < UNITS:
                    i, w, h0 = m // PAIRS, KW * (m // PAIRS + 1), m % PAIRS * 2
                    S = self.scores(m, w)
                    if m == 0:
                        place_null(c2 * 2 + s + 1, 1 - s)
                    dve.wait_ge(self.s_filled, g * UNITS + m + 1)
                    st.mark(dve.tensor_tensor(S[:, :, w - KW:w], S[:, :, w - KW:w],
                                              self.late[:, None, :].broadcast_to([P, 2, KW]), ALU.add))
                    for tile, col in ((i, 1), (i + 1, NC - 1)):
                        if tile == i and w < NC or tile > i and w == NC - KW:
                            st.mark(dve.tensor_scalar(self.s0n[s][:, tile, h0:h0 + 2], self.ps_s[m % 2][:, :, col], -SCALE,
                                                      None, ALU.mult))
                    st.wait()
                    st.mark(dve.tensor_reduce(self.mx[:, m % 2, :], S, AX, ALU.max))
                    st.wait()
                    dve.scalar_tensor_tensor(self.nm[s][:, i, h0:h0 + 2], self.mx[:, m % 2, :], -SCALE,
                                             self.s0n[s][:, i, h0:h0 + 2], ALU.mult, ALU.min)\
                        .then_inc(self.nm_ready, 1)
                if m >= 1:
                    self.pT_out(dve, dve.tensor_copy, 0, g, m - 1, self.t0_emptied)
                if m < UNITS:
                    side(g, m)
            dve.wait_ge(self.nm_ready, (g + 1) * UNITS)
            dve.tensor_tensor(self.d0[:, :, :], self.nm[s][:, :, :], self.s0n[s][:, :, :], ALU.subtract)\
                .then_inc(self.d0_ready, 1)
            dve.wait_ge(self.p0_ready, g + 1)
            st.mark(dve.tensor_tensor(self.den[:, :, :], self.rs[s][:, :, :], self.p0[:, :, :], ALU.add))
            bc = c2 * 2 + s

            def flat(a):
                return a[:, :, :].rearrange("p i h -> p (i h)")

            st.mark(dve.tensor_tensor(
                self.nulls[:, :, :].rearrange("p i (h d) -> p i h d", h=HPC),
                self.nullv[:, bass.ds(bc * P, P)].rearrange("p (a h d) -> p a h d", a=1, h=HPC).broadcast_to([P, QT, HPC, DH]),
                self.p0[:, :, :, None].broadcast_to([P, QT, HPC, DH]), ALU.mult))
            st.wait()
            st.mark(dve.reciprocal(flat(self.rden), flat(self.den)))
            dve.wait_ge(self.o_emptied, (g + 1) * QT + 2)
            st.mark(dve.tensor_tensor(self.raw[s][:, :, :], self.raw[s][:, :, :], self.nulls[:, :, :], ALU.add))
            st.wait()
            r4 = self.raw[s][:, :, :].rearrange("p i (h d) -> p (i h) d", h=HPC)
            dve.tensor_tensor(r4, r4, flat(self.rden)[:, :, None].broadcast_to([P, QT * HPC, DH]), ALU.mult)\
                .then_inc(self.raw_ready, 1)
            assert st.n == self.MARKS, st.n



PARTS = 4


def stage_b(nc, t):
    ctx = ExitStack()
    with ctx:
        sb, ps, sem = opener(nc, ctx)
        passed = t["passed"]
        att = Attention(nc, ctx, t, 0, BATCH // 2, "b_", passed)
        NE = NTILE * EXPERTS
        pos = sb("s_pos", [P, NTILE, EXPERTS])
        w = sb("s_w", [P, NTILE, EXPERTS])
        slot = sb("s_slot", [P, NTILE, EXPERTS])
        tmp = sb("s_tmp", [P, NTILE, EXPERTS])
        cnt = sb("s_cnt", [P, EXPERTS])
        cnti = sb("s_cnti", [P, EXPERTS], I32)
        nbf = sb("s_nbf", [P, EXPERTS])
        incl = sb("s_incl", [P, EXPERTS])
        start = sb("s_start", [P, EXPERTS])
        onesf = sb("s_onesf", [P, EXPERTS])
        bidx = sb("s_bidx", [P, 3])
        bcmp = sb("s_bcmp", [P, 3, EXPERTS])
        bexp = sb("s_bexp", [P, 3])
        bexpi = sb("s_bexpi", [P, 3], I32)
        lastp = sb("s_lastp", [P, 1], I32)
        s8 = sb("s_s8", [P, NTILE, TOPK])
        s8i = sb("s_s8i", [P, NTILE, TOPK], I32)
        lo = pos[:, 0:NTILE * TOPK // EXPERTS, :].rearrange("p a e -> p (a e)").bitcast(I32)
        cell = sb("s_cell", [P, NTILE * TOPK], I32)
        w8 = sb("s_w8", [P, NTILE, TOPK])
        tokens = sb("s_tokens", [P, NTILE], I32)
        zeros = sb("s_zeros", [P, NCOL], I32)
        ix = [sb(f"s_ix{r}", [P, TOPK], I32) for r in range(2)]
        tk = [sb(f"s_tk{r}", [P, 1], I32) for r in range(2)]

        tab_in = sem("s_tab_in")
        done = sem("s_done")
        w8_done = sem("s_w8_done")
        zero_ready = sem("s_zero_ready")
        ids_zeroed = sem("s_ids_zeroed")
        rows_cleared = sem("s_rows_cleared")
        tables_ready = sem("s_tables_ready")
        w8_ready = sem("s_w8_ready")
        out = sem("s_out")
        ix_ready = sem("s_ix_ready")
        scattered = [sem(f"s_scattered{r}") for r in range(2)]
        block = ctx.enter_context(nc.Block())

        @block.sync
        def _(sp):
            sp.dma_start(cnt[:, :], t["cnt"]).then_inc(tab_in, 16)
            sp.dma_start(bidx[:, :], t["bidx"]).then_inc(tab_in, 16)
            sp.dma_start(pos[:, :, :].rearrange("p a e -> p (a e)"), t["pos"]).then_inc(tab_in, 16)
            sp.dma_start(w[:, :, :].rearrange("p a e -> p (a e)"), t["w"]).then_inc(tab_in, 16)
            sp.wait_ge(zero_ready, 1)
            sp.dma_start(t["ids"].rearrange("(p n) a -> p (n a)", p=P), zeros[:, :]).then_inc(ids_zeroed, 16)

            def clear_rows(g):
                n = (NSLOT - SLOTS_USED) // att.items
                lo_ = SLOTS_USED + g * n
                sp.dma_start(t["rows"][lo_:lo_ + n, :].rearrange("(i p) c -> p i c", p=P),
                             zeros[:, None, 0:DIM].bitcast(F32).broadcast_to([P, n // P, DIM])).then_inc(rows_cleared, 16)

            att.sync(sp, clear_rows)
            sp.wait_ge(rows_cleared, 16 * att.items)
            sp.wait_ge(tables_ready, 2)
            sp.dma_start(t["used"], lastp[0:1, :]).then_inc(out, 16)
            sp.dma_start(t["blk"].rearrange("a (p j) -> (a p) j", p=P), bexpi[:, :]).then_inc(out, 16)
            sp.wait_ge(tables_ready, 3)
            sp.dma_start(t["slot8"], s8i[:, :, :].rearrange("p a k -> p (a k)")).then_inc(out, 16)
            sp.wait_ge(w8_ready, TOPK * PARTS)
            sp.dma_start(t["w8"], w8[:, :, :].rearrange("p a k -> p (a k)")).then_inc(out, 16)
            sp.wait_ge(out, 64)

        @block.gpsimd
        def _(pool):
            pool.memset(zeros[:, :], 0).then_inc(zero_ready, 1)
            pool.iota(tokens[:, :], pattern=[[P, NTILE]], base=0, channel_multiplier=1).then_inc(ix_ready, 1)
            pool.wait_ge(ids_zeroed, 16)
            pool.wait_ge(tables_ready, 3)
            hold(pool, ix_ready, 1, passed)

            def scatter(i, r, first):
                n = i * 2 + r
                if not first:
                    hold(pool, scattered[r], i * 16 * TOPK, passed)
                pool.tensor_copy(ix[r][:, :], cell[:, bass.ds(n * TOPK, TOPK)]).then_inc(ix_ready, 1)
                pool.tensor_copy(tk[r][:, :], tokens[:, bass.ds(n, 1)]).then_inc(ix_ready, 1)
                hold(pool, ix_ready, n * 2 + 3, passed)
                for k in range(TOPK):
                    pool.indirect_dma_start(t["ids"], bass.IndirectOffsetOnAxis(ap=ix[r][:, k:k + 1], axis=0), tk[r][:, :],
                                            None).then_inc(scattered[r], 16)

            for r in range(2):
                scatter(0, r, True)
            with pool.Fori(1, NTILE // 2) as i:
                for r in range(2):
                    scatter(i, r, False)
            for r in range(2):
                pool.wait_ge(scattered[r], NTILE // 2 * 16 * TOPK)

        @block.scalar
        def _(act):
            att.scalar(act)

        @block.tensor
        def _(pe):
            att.tensor(pe)

        @block.vector
        def _(dve):
            st = Steps(dve, done, 0)

            def do(instruction):
                st.mark(instruction)
                st.wait()

            dve.wait_ge(tab_in, 64)
            do(dve.memset(onesf[:, :], 1.0))
            do(dve.tensor_scalar(cnti[:, :], cnt[:, :], float(RB - 1), None, ALU.add))
            do(dve.tensor_scalar(cnti[:, :], cnti[:, :], RB.bit_length() - 1, None, ALU.logical_shift_right))
            do(dve.tensor_copy(nbf[:, :], cnti[:, :]))
            do(dve.tensor_tensor_scan(incl[:, :], onesf[:, :], nbf[:, :], 0.0, ALU.mult, ALU.add))
            do(dve.tensor_tensor(start[:, :], incl[:, :], nbf[:, :], ALU.subtract))
            do(dve.tensor_scalar(start[:, :], start[:, :], float(RB), None, ALU.mult))
            do(dve.tensor_tensor(bcmp[:, :, :], incl[:, None, :].broadcast_to([P, 3, EXPERTS]),
                                 bidx[:, :, None].broadcast_to([P, 3, EXPERTS]), ALU.is_le))
            do(dve.tensor_reduce(bexp[:, :], bcmp[:, :, :], AX, ALU.add))
            st.mark(dve.tensor_scalar(bexpi[:, :], bexp[:, :], float(EXPERTS - 1), None, ALU.min))
            st.wait()
            dve.sem_inc(tables_ready, 1)
            do(dve.tensor_scalar(lastp[:, :], incl[:, EXPERTS - 1:EXPERTS], -1.0, None, ALU.add))
            do(dve.tensor_scalar(lastp[:, :], lastp[:, :], 1, None, ALU.logical_shift_right))
            dve.sem_inc(tables_ready, 1)
            do(dve.scalar_tensor_tensor(slot[:, :, :], pos[:, :, :], 0.0,
                                        start[:, None, :].broadcast_to([P, NTILE, EXPERTS]), ALU.is_gt, ALU.mult))
            do(dve.tensor_tensor(slot[:, :, :], slot[:, :, :], pos[:, :, :], ALU.add))
            for n in range(NTILE):
                st.mark(dve.max(s8[:, n, :], slot[:, n, :]))
            st.wait()
            do(dve.tensor_scalar(s8i[:, :, :], s8[:, :, :], -1.0, None, ALU.add))
            s8f = s8i[:, :, :].rearrange("p a k -> p (a k)")
            do(dve.tensor_scalar(lo, s8f, P - 1, None, ALU.bitwise_and))
            do(dve.tensor_scalar(cell[:, :], s8f, P.bit_length() - 1, None, ALU.logical_shift_right))
            do(dve.scalar_tensor_tensor(cell[:, :], lo, float(NCOL), cell[:, :], ALU.mult, ALU.add))
            dve.sem_inc(tables_ready, 1)

            def weights(g, m):
                stage, part = m // (2 * PARTS), m % (2 * PARTS) // 2
                if m % 2 or stage > 2:
                    return
                tiles = slice(part * NTILE // PARTS, (part + 1) * NTILE // PARTS)
                shape = [P, NTILE // PARTS, EXPERTS]
                ws = Steps(dve, w8_done, g * 2 * PARTS)
                if stage:
                    ws.n = (stage - 1) * PARTS + part + 1
                    ws.wait()
                if stage == 0:
                    ws.mark(dve.tensor_tensor(tmp[:, tiles, :], slot[:, tiles, :],
                                              s8[:, tiles, bass.ds(g, 1)].broadcast_to(shape), ALU.is_equal))
                elif stage == 1:
                    ws.mark(dve.tensor_tensor(tmp[:, tiles, :], tmp[:, tiles, :], w[:, tiles, :], ALU.mult))
                else:
                    dve.tensor_reduce(w8[:, tiles, bass.ds(g, 1)], tmp[:, tiles, :], AX, ALU.add).then_inc(w8_ready, 1)

            att.vector(dve, weights)



def stage_e(nc, t):
    ctx = ExitStack()
    with ctx:
        sb, ps, sem = opener(nc, ctx, "e_")
        HC = HID // P
        GU = 2 * DC * HID
        ident = sb("ident", [P, P])
        blk = sb("blk", [1, 3 * P], I32)
        used = sb("used", [1, 1], I32)
        ids = sb("ids", [P, NCOL], I32)
        ix = [sb(f"ix{s}", [P, RT], I32) for s in range(2)]
        xg = [sb(f"xg{s}", [P, RT, DIM]) for s in range(2)]
        xT_hi = [sb(f"xT_hi{s}", [P, DC * RB], F32R) for s in range(2)]
        xT_lo = [sb(f"xT_lo{s}", [P, DC * RB], F32R) for s in range(2)]
        wgu = [sb(f"wgu{s}", [P, GU]) for s in range(2)]
        wgu_hi = [sb(f"wgu_hi{s}", [P, GU], F32R) for s in range(2)]
        wgu_lo = [sb(f"wgu_lo{s}", [P, GU], F32R) for s in range(2)]
        wd = [sb(f"wd{s}", [P, HC * DIM]) for s in range(2)]
        wd_hi = [sb(f"wd_hi{s}", [P, HC * DIM], F32R) for s in range(2)]
        wd_lo = [sb(f"wd_lo{s}", [P, HC * DIM], F32R) for s in range(2)]
        sg = [sb(f"sg{s}", [P, HC * RB]) for s in range(2)]
        gated = [sb(f"gated{s}", [P, HC * RB]) for s in range(2)]
        hT = [sb(f"hT{s}", [P, HC * RB]) for s in range(2)]
        hT_hi = [sb(f"hT_hi{s}", [P, HC * RB], F32R) for s in range(2)]
        hT_lo = [sb(f"hT_lo{s}", [P, HC * RB], F32R) for s in range(2)]
        rows = [sb(f"rows{s}", [P, RT, DIM]) for s in range(2)]
        ps_t = [ps(f"ps_t{i}", [P, DC // 2 * RB]) for i in range(2)]
        ps_g = [ps(f"ps_g{s}", [P, HC * RB]) for s in range(2)]
        ps_u = [ps(f"ps_u{s}", [P, HC * RB]) for s in range(2)]
        ps_y = [ps(f"ps_y{i}", [P, DIM]) for i in range(RT)]

        passed = t["passed"]
        const_in = sem("const_in")
        gathered = [sem(f"gathered{s}") for s in range(2)]
        gu_in = [sem(f"gu_in{s}") for s in range(2)]
        d_in = [sem(f"d_in{s}") for s in range(2)]
        ix_ready = sem("ix_ready")
        t_filled = sem("t_filled")
        xT_hi_ready = sem("xT_hi_ready")
        xT_lo_ready = sem("xT_lo_ready")
        gu_hi_ready = sem("gu_hi_ready")
        gu_lo_ready = sem("gu_lo_ready")
        d_hi_ready = sem("d_hi_ready")
        d_lo_ready = sem("d_lo_ready")
        g_filled = sem("g_filled")
        u_filled = sem("u_filled")
        sig_ready = sem("sig_ready")
        g_emptied = sem("g_emptied")
        h_ready = sem("h_ready")
        h_hi_ready = sem("h_hi_ready")
        h_lo_ready = sem("h_lo_ready")
        y_filled = sem("y_filled")
        y_emptied = sem("y_emptied")
        rows_out = [sem(f"rows_out{s}") for s in range(2)]

        def pairs(eng, step):
            last_pair = eng.value_load(used[0:1, 0:1], min_val=EXPERTS - 1, max_val=NBLK // 2 - 1)
            with eng.Fori(1, NBLK // 2 - 1) as i:
                with eng.If(i < last_pair):
                    step(i)
            return last_pair

        block = ctx.enter_context(nc.Block())

        @block.sync
        def _(sp):
            sp.dma_start(blk[:, :], t["blk"]).then_inc(const_in, 16)
            sp.dma_start(used[:, :], t["used"]).then_inc(const_in, 16)
            sp.dma_start(ident[:, :], t["ident"]).then_inc(const_in, 16)
            sp.dma_start(ids[:, :], t["ids"].rearrange("(p n) a -> p (n a)", p=P)).then_inc(const_in, 16)
            sp.wait_ge(const_in, 64)

            def load(b, s, first):
                e = sp.value_load(blk[0:1, bass.ds(b, 1)], min_val=0, max_val=EXPERTS - 1)
                if first:
                    load_gu(e, s)
                    load_d(e, s)
                    return
                before = sp.value_load(blk[0:1, bass.ds(b - 2, 1)], min_val=0, max_val=EXPERTS - 1)
                hold(sp, gu_lo_ready, b - 1, passed)
                with sp.If(e != before):
                    load_gu(e, s)
                with sp.Else():
                    sp.sem_inc(gu_in[s], 32)
                hold(sp, d_lo_ready, b - 1, passed)
                with sp.If(e != before):
                    load_d(e, s)
                with sp.Else():
                    sp.sem_inc(d_in[s], 16)

            def load_gu(e, s):
                for i, src in enumerate((t["gate_w"], t["up_w"])):
                    sp.dma_start(wgu[s][:, i * DC * HID:(i + 1) * DC * HID].rearrange("p (k h) -> p k h", h=HID),
                                 src[bass.ds(e, 1), :, :].rearrange("a (k p) h -> p (a k) h", p=P)).then_inc(gu_in[s], 16)

            def load_d(e, s):
                sp.dma_start(wd[s][:, :].rearrange("p (k c) -> p k c", c=DIM),
                             t["down_w"][bass.ds(e, 1), :, :].rearrange("a (k p) c -> p (a k) c", p=P)).then_inc(d_in[s], 16)

            def store(b, s):
                hold(sp, y_emptied, b * 2 + 4, passed)
                sp.dma_start(t["rows"][bass.ds(b * RB, RB), :].rearrange("(i p) c -> p i c", p=P), rows[s][:, :, :])\
                    .then_inc(rows_out[s], 16)

            for b in range(4):
                load(b, b % 2, b < 2)

            def step(i):
                for r in range(2):
                    load(i * 2 + 2 + r, r, False)
                    store(i * 2 - 2 + r, r)

            last_pair = pairs(sp, step)
            for b in range(-2, 2):
                store(last_pair * 2 + b, b % 2)
            for s in range(2):
                sp.wait_ge(rows_out[s], last_pair * 16 + 32)
                sp.sem_inc(passed, 1)

        @block.gpsimd
        def _(pool):
            hold(pool, const_in, 64, passed)

            def gather(b, s, first):
                if not first:
                    hold(pool, t_filled, b * 2 - 2, passed)
                pool.tensor_copy(ix[s][:, :], ids[:, bass.ds(b * RT, RT)]).then_inc(ix_ready, 1)
                hold(pool, ix_ready, b + 1, passed)
                for i in range(RT):
                    pool.indirect_dma_start(xg[s][:, i, :], None, t["xn"],
                                            bass.IndirectOffsetOnAxis(ap=ix[s][:, i:i + 1], axis=0))\
                        .then_inc(gathered[s], 16)

            def split_d(b, s, turn):
                hold(pool, d_in[s], turn * 16 + 16, passed)
                hold(pool, y_filled, b * 2 + 2, passed)
                pool.tensor_copy(wd_hi[s][:, :], wd[s][:, :]).then_inc(d_hi_ready, 1)

            gather(0, 0, True)
            gather(1, 1, True)
            for b in range(2):
                split_d(b, b, 0)
                gather(b + 2, b, False)

            def step(i):
                for s in range(2):
                    split_d(i * 2 + s, s, i)
                    gather(i * 2 + s + 2, s, False)

            last_pair = pairs(pool, step)
            for s in range(2):
                split_d(last_pair * 2 + s, s, last_pair)

        @block.scalar
        def _(act):
            act.sem_inc(y_emptied, 2)
            act.wait_ge(const_in, 64)

            def split_gu(b, s, turn, first=False):
                act.wait_ge(gu_in[s], turn * 32 + 32)
                if not first:
                    act.wait_ge(u_filled, b - 1)
                act.copy(wgu_hi[s][:, :], wgu[s][:, :]).then_inc(gu_hi_ready, 1)

            def split_x(b, s, first=False):
                for i in range(2):
                    act.wait_ge(t_filled, b * 2 + i + 1)
                    if not first:
                        act.wait_ge(u_filled, b - 1)
                    act.copy(xT_hi[s][:, i * DC // 2 * RB:(i + 1) * DC // 2 * RB], ps_t[i][:, :]).then_inc(xT_hi_ready, 1)

            def sigmoid(b, s):
                act.wait_ge(g_filled, b + 1)
                act.wait_ge(g_emptied, b + 1)
                act.activation(sg[s][:, :], ps_g[s][:, :], ACT.Sigmoid).then_inc(sig_ready, 1)

            def split_h(b, s):
                act.wait_ge(h_ready, b + 3)
                act.wait_ge(y_filled, b * 2 + 2)
                act.copy(hT_hi[s][:, :], hT[s][:, :]).then_inc(h_hi_ready, 1)

            def y_out(b, s, turn):
                act.wait_ge(rows_out[s], turn * 16 + 16)
                for i in range(RT):
                    act.wait_ge(y_filled, b * 2 + i + 5)
                    act.copy(rows[s][:, i, :], ps_y[i][:, :]).then_inc(y_emptied, 1)

            def step(b, s, turn):
                split_x(b + 1, 1 - s)
                split_h(b - 1, 1 - s)
                if not (s == 1 and isinstance(b, int) and b == 1):
                    y_out(b - 2, s, turn - 1)
                split_gu(b + 1, 1 - s, turn + s)
                sigmoid(b, s)

            split_gu(0, 0, 0, True)
            split_x(0, 0, True)
            split_gu(1, 1, 0, True)
            split_x(1, 1, True)
            sigmoid(0, 0)
            step(1, 1, 0)
            step(2, 0, 1)

            def pair(i):
                step(i * 2 + 1, 1, i)
                step(i * 2 + 2, 0, i + 1)

            last_pair = pairs(act, pair)
            b = last_pair * 2 + 1
            split_h(b - 1, 0)
            y_out(b - 2, 1, last_pair - 1)
            sigmoid(b, 1)
            split_h(b, 1)
            y_out(b - 1, 0, last_pair)
            y_out(b, 1, last_pair)

        @block.vector
        def _(dve):
            dve.sem_inc(g_emptied, 2)
            dve.sem_inc(h_ready, 2)
            for s in range(2):
                dve.sem_inc(rows_out[s], 16)
            dve.wait_ge(const_in, 64)

            def split_gu(b, s):
                dve.wait_ge(gu_hi_ready, b + 1)
                dve.tensor_tensor(wgu_lo[s][:, :], wgu[s][:, :], wgu_hi[s][:, :].bitcast(F32), ALU.subtract)\
                    .then_inc(gu_lo_ready, 1)

            def split_d(b, s):
                dve.wait_ge(d_hi_ready, b + 1)
                dve.tensor_tensor(wd_lo[s][:, :], wd[s][:, :], wd_hi[s][:, :].bitcast(F32), ALU.subtract)\
                    .then_inc(d_lo_ready, 1)

            def split_x(b, s):
                for i in range(2):
                    cols = slice(i * DC // 2 * RB, (i + 1) * DC // 2 * RB)
                    dve.wait_ge(xT_hi_ready, b * 2 + i + 1)
                    dve.tensor_tensor(xT_lo[s][:, cols], ps_t[i][:, :], xT_hi[s][:, cols].bitcast(F32), ALU.subtract)\
                        .then_inc(xT_lo_ready, 1)

            def hidden(b, s):
                dve.wait_ge(sig_ready, b + 1)
                dve.tensor_tensor(gated[s][:, :], sg[s][:, :], ps_g[s][:, :], ALU.mult).then_inc(g_emptied, 1)
                dve.wait_ge(u_filled, b + 1)
                dve.wait_ge(g_emptied, b + 3)
                dve.tensor_tensor(hT[s][:, :], gated[s][:, :], ps_u[s][:, :], ALU.mult).then_inc(h_ready, 1)

            def split_h(b, s):
                dve.wait_ge(h_hi_ready, b + 1)
                dve.tensor_tensor(hT_lo[s][:, :], hT[s][:, :], hT_hi[s][:, :].bitcast(F32), ALU.subtract)\
                    .then_inc(h_lo_ready, 1)

            def step(b, s):
                hidden(b - 1, 1 - s)
                split_x(b + 1, 1 - s)
                split_h(b - 1, 1 - s)
                split_gu(b + 1, 1 - s)
                split_d(b, s)

            for b in range(2):
                split_gu(b, b)
                split_x(b, b)
            split_d(0, 0)
            step(1, 1)
            step(2, 0)

            def pair(i):
                step(i * 2 + 1, 1)
                step(i * 2 + 2, 0)

            last_pair = pairs(dve, pair)
            b = last_pair * 2 + 1
            hidden(b - 1, 0)
            split_h(b - 1, 0)
            split_d(b, 1)
            hidden(b, 1)
            split_h(b, 1)

        @block.tensor
        def _(pe):
            pe.sem_inc(y_filled, 4)
            pe.wait_ge(const_in, 64)

            def transposes(b, s, turn, first=False):
                hold(pe, gathered[s], (turn + 1) * 16 * RT, passed)
                for k in range(DC):
                    if k % 2 == 0 and not first:
                        pe.wait_ge(xT_lo_ready, b * 2 - 1 + k // 2)
                    for i in range(RT):
                        o = k % 2 * RB + i * P
                        last = pe.transpose(ps_t[k // 2][:, o:o + P], xg[s][:, i, k * P:(k + 1) * P], ident[:, :])
                    if k % 2:
                        last.then_inc(t_filled, 1)

            def gate_up(b, s):
                pe.wait_ge(gu_lo_ready, b + 1)
                pe.wait_ge(xT_lo_ready, b * 2 + 2)
                for kind, (dst, free, filled) in enumerate(((ps_g, g_emptied, g_filled), (ps_u, h_ready, u_filled))):
                    pe.wait_ge(free, b + 1)
                    for h in range(HC):
                        for k in range(DC):
                            w0, x0 = (kind * DC + k) * HID + h * P, k * RB
                            for n, (w, x) in enumerate(((wgu_hi, xT_hi), (wgu_hi, xT_lo), (wgu_lo, xT_hi))):
                                last = pe.matmul(dst[s][:, h * RB:(h + 1) * RB], w[s][:, w0:w0 + P], x[s][:, x0:x0 + RB],
                                                 start=k == 0 and n == 0, stop=k == DC - 1 and n == 2)
                    last.then_inc(filled, 1)

            def down(b, s):
                pe.wait_ge(d_lo_ready, b + 1)
                pe.wait_ge(h_lo_ready, b + 1)
                for i in range(RT):
                    pe.wait_ge(y_emptied, b * 2 + i + 1)
                    for h in range(HC):
                        h0 = h * RB + i * P
                        for n, (x, w) in enumerate(((hT_hi, wd_hi), (hT_hi, wd_lo), (hT_lo, wd_hi))):
                            last = pe.matmul(ps_y[i][:, :], x[s][:, h0:h0 + P], w[s][:, h * DIM:(h + 1) * DIM],
                                             start=h == 0 and n == 0, stop=h == HC - 1 and n == 2)
                    last.then_inc(y_filled, 1)

            def step(b, s, turn):
                transposes(b + 1, 1 - s, turn + s)
                gate_up(b, s)
                down(b - 1, 1 - s)

            transposes(0, 0, 0, True)
            transposes(1, 1, 0)
            gate_up(0, 0)
            step(1, 1, 0)
            step(2, 0, 1)

            def pair(i):
                step(i * 2 + 1, 1, i)
                step(i * 2 + 2, 0, i + 1)

            last_pair = pairs(pe, pair)
            b = last_pair * 2 + 1
            gate_up(b, 1)
            down(b - 1, 0)
            down(b, 1)



def stage_f(nc, t):
    ctx = ExitStack()
    with ctx:
        sb, ps, sem = opener(nc, ctx, "f_")
        passed = t["passed"]
        att = Attention(nc, ctx, t, BATCH // 2, BATCH // 2, "g_", passed)
        TPI = NTILE // att.items
        slots = sb("slots", [P, NTILE * TOPK], I32)
        w8 = sb("w8", [P, NTILE * TOPK])
        ix = [sb(f"ix{r}", [P, TOPK], I32) for r in range(2)]
        xs = [sb(f"xs{r}", [P, 2, DIM]) for r in range(2)]
        got = [sb(f"got{r}", [P, TOPK, DIM]) for r in range(2)]
        acc = [sb(f"acc{r}", [P, DIM]) for r in range(2)]

        tab_in = sem("tab_in")
        xs_in = [sem(f"xs_in{r}") for r in range(2)]
        ix_ready = sem("ix_ready")
        gathered = [sem(f"gathered{r}") for r in range(2)]
        step_done = sem("step_done")
        acc_ready = sem("acc_ready")
        base_out = [sem(f"base_out{r}") for r in range(2)]
        block = ctx.enter_context(nc.Block())

        @block.sync
        def _(sp):
            sp.dma_start(slots[:, :], t["slot8"]).then_inc(tab_in, 16)
            sp.dma_start(w8[:, :], t["w8"]).then_inc(tab_in, 16)

            def load(n, r):
                sp.dma_start(xs[r][:, 0, :], t["x"][bass.ds(n * P, P), :]).then_inc(xs_in[r], 16)
                sp.dma_start(xs[r][:, 1, :], t["shared"][bass.ds(n * P, P), :]).then_inc(xs_in[r], 16)

            def tiles(g):
                def one(n, r, load_too):
                    hold(sp, acc_ready, n + 1, passed)
                    if load_too:
                        load(n + 2, r)
                    sp.dma_start(t["base"][bass.ds(n * P, P), :], acc[r][:, :]).then_inc(base_out[r], 16)

                full = g < att.items - 1
                with sp.Fori(0, TPI // 2 - (0 if full else 1)) as i:
                    for r in range(2):
                        one(i * 2 + g * TPI + r, r, True)
                if not full:
                    for r in range(2):
                        one(NTILE - 2 + r, r, False)

            load(0, 0)
            load(1, 1)
            att.sync(sp, tiles)
            for r in range(2):
                sp.wait_ge(base_out[r], 16 * (NTILE // 2 + 1))

        @block.gpsimd
        def _(pool):
            hold(pool, tab_in, 32, passed)

            def gather(i, r, first):
                n = i * 2 + r
                if not first:
                    hold(pool, acc_ready, n - 1, passed)
                pool.tensor_copy(ix[r][:, :], slots[:, bass.ds(n * TOPK, TOPK)]).then_inc(ix_ready, 1)
                hold(pool, ix_ready, n + 1, passed)
                for k in range(TOPK):
                    pool.indirect_dma_start(got[r][:, k, :], None, t["rows"],
                                            bass.IndirectOffsetOnAxis(ap=ix[r][:, k:k + 1], axis=0))\
                        .then_inc(gathered[r], 16)

            for r in range(2):
                gather(0, r, True)
            with pool.Fori(1, NTILE // 2) as i:
                for r in range(2):
                    gather(i, r, False)

        @block.scalar
        def _(act):
            att.scalar(act)

        @block.tensor
        def _(pe):
            att.tensor(pe)

        @block.vector
        def _(dve):
            for r in range(2):
                dve.sem_inc(base_out[r], 16)
            dve.wait_ge(tab_in, 32)

            def combine(g, m):
                f, part = m // CALLS, m % CALLS
                r = f % 2
                n = g * TPI + f
                turn_ = g * (TPI // 2) + f // 2
                st = Steps(dve, step_done, n * TOPK)
                if part == 0:
                    dve.wait_ge(xs_in[r], turn_ * 32 + 32)
                    dve.wait_ge(base_out[r], turn_ * 16 + 16)
                    st.mark(dve.tensor_tensor(acc[r][:, :], xs[r][:, 0, :], xs[r][:, 1, :], ALU.add))
                    dve.wait_ge(gathered[r], turn_ * (16 * TOPK) + 16 * TOPK)
                for k in range(part * TOPK // CALLS, (part + 1) * TOPK // CALLS):
                    st.n = k + 1
                    st.wait()
                    last = dve.scalar_tensor_tensor(acc[r][:, :], got[r][:, k, :], w8[:, bass.ds(n * TOPK + k, 1)],
                                                    acc[r][:, :], ALU.mult, ALU.add)
                    if k < TOPK - 1:
                        last.then_inc(step_done, 1)
                if part == CALLS - 1:
                    last.then_inc(acc_ready, 1)

            CALLS = UNITS // TPI
            att.vector(dve, combine)



def stage_c(nc, t):
    ctx = ExitStack()
    with ctx:
        sb, ps, sem = opener(nc, ctx, "c_")
        HT = SEQ // 2 // P
        NP = BATCH * HT
        NCOS, NSIN = DIM // 2 + 1, DIM // 2 - 1
        MB = SEQ // 4 // P
        wout = sb("wout", [P, DC, DIM])
        dft = sb("dft", [P, DC, DIM])
        w2 = sb("w2", [P, DC, DIM])
        bcol = sb("bcol", [P, DC])
        brep = sb("brep", [P, DC, P])
        b2 = sb("b2", [P, DIM])
        ident = sb("ident", [P, P])
        alt = sb("alt", [P, 1])
        att = sb("att", [P, 2, DIM])
        sd = [sb(f"sd{v}", [P, DIM]) for v in range(2)]
        sdT = [sb(f"sdT{v}", [P, DC, P]) for v in range(2)]
        y = [sb(f"y{v}", [P, NP, DIM]) for v in range(2)]
        qs = [sb(f"qs{r}", [P, NCOS]) for r in range(2)]
        dif = [sb(f"dif{r}", [P, NCOS]) for r in range(2)]
        turned = [sb(f"turned{r}", [P, DIM]) for r in range(2)]
        flip = sb("flip", [P, P])
        base = [[sb(f"base{v}{r}", [P, DIM]) for r in range(2)] for v in range(2)]
        ps_t = [ps(f"ps_t{v}", [P, DIM]) for v in range(2)]
        ps_y = [ps(f"ps_y{v}", [P, DIM]) for v in range(2)]
        ps_p = [ps(f"ps_p{r}", [P, 512]) for r in range(2)]
        ps_q = [ps(f"ps_q{r}", [P, 512]) for r in range(2)]
        cos = [wout, dft]
        sin = [sb(f"sin{v}", [P, HT, P]) for v in range(2)]
        cos = [c[:, :, :].rearrange("p k n -> p (k n)")[:, 0:HT * P].rearrange("p (k n) -> p k n", k=HT) for c in cos]

        passed = t["passed"]
        const_in = sem("const_in")
        brep_ready = sem("brep_ready")
        att_in = sem("att_in")
        sd_ready = sem("sd_ready")
        w_filled = sem("w_filled")
        w_emptied = sem("w_emptied")
        t_filled = sem("t_filled")
        t_emptied = sem("t_emptied")
        y_filled = sem("y_filled")
        y_emptied = sem("y_emptied")
        tab_in = [sem(f"tab_in{v}") for v in range(2)]
        p_filled = sem("p_filled")
        q_filled = sem("q_filled")
        p_emptied = sem("p_emptied")
        q_emptied = sem("q_emptied")
        dve_done = sem("dve_done")
        qs_zeroed = sem("qs_zeroed")
        base_in = [sem(f"base_in{r}") for r in range(2)]
        turned_ready = sem("turned_ready")
        r_filled = sem("r_filled")
        out_ready = sem("out_ready")
        out_done = [sem(f"out_done{r}") for r in range(2)]
        last_in = sem("last_in")
        last_filled = sem("last_filled")
        last_ready = sem("last_ready")
        last_done = sem("last_done")
        block = ctx.enter_context(nc.Block())

        U = 2 * BATCH
        NU = MB * U

        @block.sync
        def _(sp):
            for dst, src in ((wout, t["wout_t"]), (dft, t["dft_d"])):
                sp.dma_start(dst[:, :, :], src.rearrange("(k p) n -> p k n", p=P)).then_inc(const_in, 16)
            for dst, src in ((bcol, t["b_out_col"]), (ident, t["ident"]), (alt, t["alt"]), (flip, t["flip"])):
                sp.dma_start(dst[:, :], src).then_inc(const_in, 16)
            with sp.Fori(0, BATCH) as b:
                with sp.Fori(0, HT) as i:
                    hold(sp, sd_ready, (b * HT + i) * 2 + 2, passed)
                    for v in range(2):
                        sp.dma_start(att[:, v, :], t["att"][bass.ds(b * SEQ + i * P + v * HT * P, P), :]).then_inc(att_in, 16)

            def unit(n):
                m, v, b = n // U, n // BATCH % 2, n % BATCH
                k1 = [b * SEQ + (m * P + p) * 2 + v for p in (0, P - 1)]
                rows = P - 1 if (m, v) == (0, 0) else P
                up = t["base"][k1[0]:k1[1] + 1:2, :], t["out"][k1[0]:k1[1] + 1:2, :]
                lo = (2 * b + 1) * SEQ - k1[1]
                down = [a[lo:lo + 2 * rows - 1:2, :] for a in (t["base"], t["out"])]
                return rows, up, down

            def load_base(n):
                r = n % 2
                rows, up, down = unit(n)
                if n >= 2:
                    sp.wait_ge(out_done[r], 32 * (n // 2))
                sp.dma_start(base[0][r][:, :], up[0]).then_inc(base_in[r], 16)
                sp.dma_start(base[1][r][0:rows, :], down[0]).then_inc(base_in[r], 16)

            def load_tables(m, v):
                if (m, v) == (0, 0):
                    sp.wait_ge(w_filled, DC + 1)
                if m:
                    sp.wait_ge(q_filled, (m - 1) * U + (v + 1) * BATCH)
                sp.dma_start(cos[v], t["cos_t"][v, m, :, :, :]).then_inc(tab_in[v], 16)
                sp.dma_start(sin[v][:, :, :], t["sin_t"][v, m, :, :, :]).then_inc(tab_in[v], 16)

            for v in range(2):
                load_tables(0, v)
            sp.wait_ge(qs_zeroed, 1)
            load_base(0)
            load_base(1)
            for n in range(NU):
                sp.wait_ge(out_ready, n + 1)
                r = n % 2
                rows, up, down = unit(n)
                sp.dma_start(up[1], base[0][r][:, :]).then_inc(out_done[r], 16)
                sp.dma_start(down[1], base[1][r][0:rows, :]).then_inc(out_done[r], 16)
                if n % BATCH == BATCH - 1 and n // U + 1 < MB:
                    load_tables(n // U + 1, n // BATCH % 2)
                if n + 2 < NU:
                    load_base(n + 2)
            for r in range(2):
                sp.wait_ge(out_done[r], 16 * NU)
            for b in range(BATCH):
                row = b * SEQ + SEQ // 2
                sp.dma_start(base[b // 2][b % 2][0:1, :], t["base"][row:row + 1, :]).then_inc(last_in, 16)
            sp.wait_ge(last_in, 16 * BATCH)
            sp.wait_ge(last_ready, 1)
            for b in range(BATCH):
                row = b * SEQ + SEQ // 2
                sp.dma_start(t["out"][row:row + 1, :], base[b // 2][b % 2][0:1, :]).then_inc(last_done, 16)
            sp.wait_ge(last_done, 16 * BATCH)

        @block.tensor
        def _(pe):
            pe.wait_ge(const_in, 16 * 6)
            for m in range(DC + 1):
                dst = (ps_p + ps_q + ps_y[:1])[m]
                if m == DC:
                    pe.wait_ge(brep_ready, 1)
                for k in range(DC):
                    lhs = wout[:, k, m * P:(m + 1) * P] if m < DC else brep[:, k, :]
                    last = pe.matmul(dst[:, :], lhs, dft[:, k, :], start=k == 0, stop=k == DC - 1)
                last.then_inc(w_filled, 1)
            pe.wait_ge(w_emptied, DC + 1)

            def transposes(n, v):
                pe.wait_ge(t_emptied, n * 2 + v + 1)
                hold(pe, sd_ready, n * 2 + v + 3, passed)
                for k in range(DC):
                    last = pe.transpose(ps_t[v][:, k * P:(k + 1) * P], sd[v][:, k * P:(k + 1) * P], ident[:, :])
                last.then_inc(t_filled, 1)

            def project(n, v):
                pe.wait_ge(t_emptied, n * 2 + v + 3)
                pe.wait_ge(y_emptied, n * 2 + v + 1)
                for k in range(DC):
                    last = pe.matmul(ps_y[v][:, :], sdT[v][:, k, :], w2[:, k, :], start=k == 0, stop=k == DC - 1)
                last.then_inc(y_filled, 1)

            transposes(0, 0)
            with pe.Fori(0, NP - 1) as n:
                transposes(n, 1)
                project(n, 0)
                transposes(n + 1, 0)
                project(n, 1)
            transposes(NP - 1, 1)
            project(NP - 1, 0)
            project(NP - 1, 1)
            pe.wait_ge(y_emptied, NP * 2 + 2)

            def turn_rows(n, r):
                pe.wait_ge(turned_ready, n + 1)
                pe.matmul(ps_t[r][:, :], flip[:, :], turned[r][:, :], start=True, stop=True).then_inc(r_filled, 1)

            def chunk(m, first):
                for v in range(2):
                    pe.wait_ge(tab_in[v], m * 32 + 32)
                    for b in range(BATCH):
                        n = m * U + v * BATCH + b
                        for table, dst, c0, c1, free, filled in (
                                (cos[v], ps_p, 0, NCOS, p_emptied, p_filled),
                                (sin[v][:, :, :], ps_q, NCOS, DIM, q_emptied, q_filled)):
                            pe.wait_ge(free, n + 1)
                            for k in range(HT):
                                last = pe.matmul(dst[b % 2][:, 0:c1 - c0], table[:, k, :], y[v][:, b * HT + k, c0:c1],
                                                 start=k == 0, stop=k == HT - 1)
                            last.then_inc(filled, 1)
                        if v or b or not first:
                            turn_rows(n - 1, (b + 1) % 2)

            chunk(0, True)
            with pe.Fori(1, MB) as m:
                chunk(m, False)
            turn_rows(NU - 1, 1)
            pe.wait_ge(p_emptied, NU + 2)
            pe.wait_ge(q_emptied, NU + 2)
            for b in range(BATCH):
                dst = (ps_p + ps_q)[b]
                for k in range(HT):
                    last = pe.matmul(dst[0:1, 0:NCOS], alt[:, :], y[0][:, b * HT + k, 0:NCOS], start=k == 0,
                                     stop=k == HT - 1)
            last.then_inc(last_filled, 1)

        @block.scalar
        def _(act):
            act.sem_inc(q_emptied, 2)
            act.sem_inc(t_emptied, 2)
            for m in range(DC + 1):
                act.wait_ge(w_filled, m + 1)
                src = (ps_p + ps_q + ps_y[:1])[m]
                act.activation(w2[:, m, :] if m < DC else b2[:, :], src[:, :], ACT.Copy, scale=1.0 if m < DC else 2.0)\
                    .then_inc(w_emptied, 1)
            with act.Fori(0, NP) as n:
                for v in range(2):
                    act.wait_ge(t_filled, n * 2 + v + 1)
                    act.wait_ge(y_filled, n * 2 + v + 1)
                    act.copy(sdT[v][:, :, :].rearrange("p k n -> p (k n)"), ps_t[v][:, :]).then_inc(t_emptied, 1)
            act.wait_ge(qs_zeroed, 1)
            with act.Fori(0, NU // 2) as i:
                for r in range(2):
                    act.wait_ge(q_filled, i * 2 + r + 1)
                    act.wait_ge(p_emptied, i * 2 + r + 1)
                    act.copy(qs[r][:, 1:1 + NSIN], ps_q[r][:, 0:NSIN]).then_inc(q_emptied, 1)

        @block.vector
        def _(dve):
            dve.sem_inc(sd_ready, 2)
            dve.sem_inc(y_emptied, 2)
            dve.sem_inc(y_filled, 2)
            dve.sem_inc(p_emptied, 2)
            for r in range(2):
                dve.memset(qs[r][:, :], 0.0)
                last = dve.memset(base[1][r][:, :], 0.0)
            last.then_inc(qs_zeroed, 1)
            dve.wait_ge(const_in, 16 * 6)
            dve.tensor_copy(brep[:, :, :], bcol[:, :, None].broadcast_to([P, DC, P])).then_inc(brep_ready, 1)
            dve.wait_ge(w_emptied, DC + 1)
            def halves(n):
                dve.wait_ge(att_in, n * 32 + 32)
                for v, op in ((0, ALU.add), (1, ALU.subtract)):
                    dve.wait_ge(t_filled, n * 2 + v - 1) if not isinstance(n, int) or n else None
                    dve.tensor_tensor(sd[v][:, :], att[:, 0, :], att[:, 1, :], op).then_inc(sd_ready, 1)

            def project_out(n):
                for v in range(2):
                    dve.wait_ge(y_filled, n * 2 + v + 3)
                    dst = y[v][:, bass.ds(n, 1), :].rearrange("p a c -> p (a c)")
                    if v:
                        dve.tensor_copy(dst, ps_y[v][:, :]).then_inc(y_emptied, 1)
                    else:
                        dve.tensor_tensor(dst, ps_y[v][:, :], b2[:, :], ALU.add).then_inc(y_emptied, 1)

            halves(0)
            with dve.Fori(1, NP) as n:
                halves(n)
                project_out(n - 1)
            project_out(NP - 1)

            def mirror(z):
                return z[:, 1:1 + NSIN][:, ::-1]

            def rows_up(n, r, turn_):
                st = Steps(dve, dve_done, n * 4)
                dve.wait_ge(p_filled, n + 1)
                dve.wait_ge(q_emptied, n + 3)
                st.mark(dve.tensor_tensor(dif[r][:, :], ps_p[r][:, 0:NCOS], qs[r][:, :], ALU.subtract))
                dve.tensor_tensor(turned[r][:, 0:NCOS], ps_p[r][:, 0:NCOS], qs[r][:, :], ALU.add).then_inc(p_emptied, 1)
                st.wait()
                st.mark(dve.tensor_copy(turned[r][:, NCOS:DIM], mirror(dif[r])))
                dve.wait_ge(p_emptied, n + 3)
                st.wait()
                dve.sem_inc(turned_ready, 1)
                dve.wait_ge(base_in[r], turn_ * 32 + 32)
                up = base[0][r]
                st.mark(dve.tensor_tensor(up[:, 0:NCOS], up[:, 0:NCOS], dif[r][:, :], ALU.add))
                st.mark(dve.tensor_tensor(up[:, NCOS:DIM], up[:, NCOS:DIM], mirror(turned[r]), ALU.add))
                st.wait()

            def rows_down(n, r):
                dve.wait_ge(r_filled, n + 1)
                dve.tensor_tensor(base[1][r][:, :], base[1][r][:, :], ps_t[r][:, :], ALU.add).then_inc(out_ready, 1)

            rows_up(0, 0, 0)
            with dve.Fori(0, NU // 2 - 1) as i:
                rows_up(i * 2 + 1, 1, i)
                rows_down(i * 2, 0)
                rows_up(i * 2 + 2, 0, i + 1)
                rows_down(i * 2 + 1, 1)
            rows_up(NU - 1, 1, NU // 2 - 1)
            rows_down(NU - 2, 0)
            rows_down(NU - 1, 1)
            dve.wait_ge(last_filled, 1)
            dve.wait_ge(last_in, 16 * BATCH)
            st = Steps(dve, dve_done, NU * 4)
            for b in range(BATCH):
                row, src = base[b // 2][b % 2], (ps_p + ps_q)[b]
                st.mark(dve.tensor_tensor(row[0:1, 0:NCOS], row[0:1, 0:NCOS], src[0:1, 0:NCOS], ALU.add))
                st.mark(dve.tensor_tensor(row[0:1, NCOS:DIM], row[0:1, NCOS:DIM], src[0:1, 1:1 + NSIN][:, ::-1], ALU.add))
            st.wait()
            dve.sem_inc(last_ready, 1)
def internal(nc):
    def d(name, shape, dt=F32):
        return nc.dram_tensor(f"mid_{name}", shape, dt, kind="Internal").ap()

    return dict(
        xn=d("xn", (TOK, DIM)), q_hi=d("q_hi", (DC, P, TOK)), q_lo=d("q_lo", (DC, P, TOK)),
        kc_hi=d("kc_hi", (DC, P, TOK // CF)), kc_lo=d("kc_lo", (DC, P, TOK // CF)), vc=d("vc", (TOK // CF, DIM)),
        shared=d("shared", (TOK, DIM)), w=d("w", (P, NTILE * EXPERTS)), pos=d("pos", (P, NTILE * EXPERTS)),
        cnt=d("cnt", (P, EXPERTS)), ids=d("ids", (NSLOT, 1), I32), blk=d("blk", (1, 3 * P), I32), used=d("used", (1, 1), I32),
        slot8=d("slot8", (P, NTILE * TOPK), I32), w8=d("w8", (P, NTILE * TOPK)), rows=d("rows", (NSLOT, DIM)),
        att=d("att", (TOK, DIM)), base=d("base", (TOK, DIM)), passed=nc.alloc_semaphore("passed"))


def layout(L0_attn_x, L0_attn_Wqkv, L0_attn_conv_w, L0_attn_conv_b, L0_attn_null_k, L0_attn_null_v, L0_attn_W_out,
           L0_attn_b_out, L0_ffn_router_w, L0_ffn_e_bias, L0_ffn_gate_w, L0_ffn_up_w, L0_ffn_down_w, L0_ffn_sh_gate_w,
           L0_ffn_sh_up_w, L0_ffn_sh_down_w):
    def a(v):
        return np.ascontiguousarray(np.asarray(v, dtype=np.float32))

    def rows(v):
        return np.ascontiguousarray(np.broadcast_to(a(v).reshape(1, -1), (P, a(v).size)))

    conv = a(L0_attn_conv_w).reshape(DC, HPC, DH, DH, CF)
    conv_bd = np.zeros((P, DC, CF, P), np.float32)
    null_k = a(L0_attn_null_k).reshape(DC, HPC, DH)
    null_rows = np.zeros((3, DH, DC + 1, HPC, 2), np.float32)
    for h in range(HPC):
        s = slice(h * DH, (h + 1) * DH)
        conv_bd[s, :, :, s] = conv[:, h].transpose(2, 0, 3, 1)
    null_rows[:] = null_k[[*range(DC), 0]].transpose(2, 0, 1)[None, :, :, :, None]
    tt = np.arange(SEQ // 2, dtype=np.float64)[:, None]
    k1 = np.arange(SEQ // 2 + 1, dtype=np.float64)[None, :]
    ang = 2 * np.pi * ((tt * k1) % SEQ) / SEQ
    ee = np.arange(DIM, dtype=np.float64)[:, None]
    angd = 2 * np.pi * ((ee * np.arange(DIM // 2 + 1)[None, :]) % DIM) / DIM
    dft_d = np.concatenate([np.cos(angd), np.sin(angd[:, 1:DIM // 2])], axis=1).astype(np.float32)
    def tables(f):
        m = f(ang)[:, :SEQ // 2].reshape(SEQ // 2 // P, P, SEQ // 4 // P, P, 2)
        return np.ascontiguousarray(m.transpose(4, 2, 1, 0, 3)).astype(np.float32)
    return dict(
        x=a(L0_attn_x).reshape(TOK, DIM), wqkv=a(L0_attn_Wqkv), conv_bd=conv_bd,
        conv_b_col=np.ascontiguousarray(a(L0_attn_conv_b).reshape(DC, P).T), conv_b_row=rows(L0_attn_conv_b),
        null_rows=null_rows.reshape(3 * DH, (DC + 1) * HPC * 2), null_v_row=rows(L0_attn_null_v), wout_t=np.ascontiguousarray(a(L0_attn_W_out).T),
        b_out_col=np.ascontiguousarray(a(L0_attn_b_out).reshape(DC, P).T),
        router_t=np.ascontiguousarray(a(L0_ffn_router_w).T), e_bias_row=rows(L0_ffn_e_bias),
        gate_w=a(L0_ffn_gate_w), up_w=a(L0_ffn_up_w), down_w=a(L0_ffn_down_w),
        sh_gate=a(L0_ffn_sh_gate_w), sh_up=a(L0_ffn_sh_up_w), sh_down=a(L0_ffn_sh_down_w),
        ident=np.eye(P, dtype=np.float32), tri=np.triu(np.ones((P, P), np.float32), 1), ones=np.ones((P, P), np.float32),
        before=np.ascontiguousarray(np.broadcast_to(np.tril(np.ones((GROUPS, GROUPS), np.float32), -1), (P, GROUPS, GROUPS))),
        bidx=np.arange(3 * P, dtype=np.float32).reshape(P, 3),
        mhalf=np.full((P, TPB), -0.5, np.float32),
        late=np.where(np.arange(P)[:, None] >= CF * np.arange(P // CF)[None, :] + CF - 1, 0.0, -BIG).astype(np.float32),
        cos_t=tables(np.cos), sin_t=tables(np.sin),
        alt=np.ascontiguousarray(np.broadcast_to(np.where(np.arange(P) % 2, -1.0, 1.0)[:, None], (P, 1))).astype(np.float32),
        flip=np.ascontiguousarray(np.eye(P, dtype=np.float32)[::-1]), dft_d=dft_d)


def program(nc, t):
    stage_a(nc, t)
    stage_b(nc, t)
    stage_e(nc, t)
    stage_f(nc, t)
    stage_c(nc, t)


def kernel(**inputs):
    import concourse.bacc as bacc
    from concourse.bass_utils import run_bass_kernel_spmd

    nc = bacc.Bacc("TRN2", target_bir_lowering=False, num_devices=1)
    arrays, aps = {}, internal(nc)
    for name, a in layout(**inputs).items():
        arrays[f"in_{name}"] = a
        aps[name] = nc.dram_tensor(f"in_{name}", a.shape, mybir.dt.from_np(a.dtype), kind="ExternalInput").ap()
    aps["out"] = nc.dram_tensor("out", (TOK, DIM), F32, kind="ExternalOutput").ap()
    program(nc, aps)
    r = run_bass_kernel_spmd(nc, [arrays], core_ids=[0])
    return r.results[0]["out"].reshape(BATCH, SEQ, DIM)
```
